# Optimizing a Trainium2 kernel written in Bass

```python
import numpy as np
import jax
import jax.numpy as jnp

def _softmax(x, axis=-1):
    return jax.nn.softmax(x, axis=axis)

def _gelu(x):
    return jax.nn.gelu(x, approximate=True)

def _silu(x):
    return jax.nn.silu(x)

def _sigmoid(x):
    return jax.nn.sigmoid(x)

def _layernorm(x, axis=-1, eps=1e-05):
    m = jnp.mean(x, axis=axis, keepdims=True)
    v = jnp.var(x, axis=axis, keepdims=True)
    return (x - m) / jnp.sqrt(v + eps)

def _scatter_add(tgt, idx, src, axis=0):
    return tgt.at[idx].add(src)

def _segment_sum(src, seg, n):
    return jax.ops.segment_sum(src, seg, n)
kernel_name = 'mk_xattn_ffn_d1_seqx_r4_4e300c'

def setup_inputs(seed: int=0):
    np.random.seed(seed)
    _w = jnp.asarray

    def _rec_inputs():
        import jax
        import jax.numpy as jnp
        _rk = jax.random.key(seed)
        x = 7.22e-05 + 1 * jax.random.normal(jax.random.fold_in(_rk, 1), (16, 100, 512), jnp.float32)
        _lenS = 100 - jax.random.randint(jax.random.fold_in(_rk, 7), (16,), 0, max(1, 100 // 4) + 1, jnp.int32)
        _lenS2 = 361 - jax.random.randint(jax.random.fold_in(_rk, 8), (16,), 0, max(1, 361 // 4) + 1, jnp.int32)
        _ctx_2048P = jax.random.normal(jax.random.fold_in(_rk, 11), (16, 16, 512), jnp.float32)
        _ctx_2048c = jax.random.dirichlet(jax.random.fold_in(_rk, 511), 0.3 * jnp.ones((16,), jnp.float32), (16, 361))
        _ctx_2048t = jnp.einsum('bsk,bkd->bsd', _ctx_2048c, _ctx_2048P)
        _ctx_2048t = _ctx_2048t * jax.lax.rsqrt(jnp.mean(jnp.square(_ctx_2048t)) + 1e-12) * 0.953939
        ctx_2048 = 4.13588e-05 + 0.999923 * (_ctx_2048t + 0.3 * jax.random.normal(jax.random.fold_in(_rk, 611), (16, 361, 512), jnp.float32))
        _validS = jnp.arange(100)[None, :] < _lenS[:, None]
        _validS2 = jnp.arange(361)[None, :] < _lenS2[:, None]
        _causal = jnp.tril(jnp.ones((100, 100), dtype=bool))
        mask_BxS2_bf1 = jnp.ones((16, 361), dtype=bool)
        return (x, ctx_2048, mask_BxS2_bf1)
    x, ctx_2048, mask_BxS2_bf1 = _rec_inputs()

    def _L0_xattn_setup():
        import jax, jax.numpy as jnp
        import numpy as np
        import math
        D_MODEL = 512
        N_Q_HEADS = 16
        N_KV_HEADS = 4
        HEAD_DIM = D_MODEL // N_Q_HEADS
        B = 4
        S = 256

        def _alibi_slopes(num_heads):
            n = 2 ** int(math.floor(math.log2(num_heads)))
            m0 = 2.0 ** (-8.0 / n)
            return m0 ** jnp.arange(1, n + 1, dtype=jnp.float32)
        key = jax.random.key(seed)
        ks = jax.random.split(key, 8)
        xavier = lambda k, fi, fo: jax.random.normal(k, (fi, fo), jnp.float32) * math.sqrt(2.0 / (fi + fo))
        return {'query': jax.random.normal(ks[0], (B, S, D_MODEL), jnp.float32), 'key': jax.random.normal(ks[1], (B, S, D_MODEL), jnp.float32), 'value': jax.random.normal(ks[2], (B, S, D_MODEL), jnp.float32), 'mask': jnp.ones((B, S), dtype=bool), 'Wq': xavier(ks[3], D_MODEL, N_Q_HEADS * HEAD_DIM), 'Wk': xavier(ks[4], D_MODEL, N_KV_HEADS * HEAD_DIM), 'Wv': xavier(ks[5], D_MODEL, N_KV_HEADS * HEAD_DIM), 'Wo': xavier(ks[6], D_MODEL, D_MODEL)}
    _L0_xattn_all = _L0_xattn_setup()
    _L0_xattn_in = {k: v for k, v in _L0_xattn_all.items() if k in ('Wq', 'Wk', 'Wv', 'Wo')}
    del _L0_xattn_all

    def _L0_ffn_setup():
        import jax, jax.numpy as jnp
        import numpy as np
        GROUP_SIZE = 64

        def ternary_quant(w_fp32, g=GROUP_SIZE):
            w = w_fp32.astype(jnp.bfloat16)
            w_g = w.reshape(-1, g)
            scale = jnp.clip(jnp.mean(jnp.abs(w_g), axis=-1, keepdims=True), 1e-08, None)
            q = jnp.clip(jnp.round(w_g / scale), -1, 1)
            w_hat = (q * scale).reshape(w.shape)
            return w + jax.lax.stop_gradient(w_hat - w)

        def rms_norm(x):
            eps = jnp.finfo(x.dtype).eps.astype(jnp.float32)
            xf = x.astype(jnp.float32)
            inv = jax.lax.rsqrt(jnp.mean(xf * xf, axis=-1, keepdims=True) + eps)
            return (xf * inv).astype(x.dtype)
        key = jax.random.key(seed)
        k1, k2, k3 = jax.random.split(key, 3)
        B, S, D = (2, 512, 512)
        H = 4 * D
        x = jax.random.normal(k1, (B, S, D), dtype=jnp.float32).astype(jnp.bfloat16)
        w_gate_up = jax.random.normal(k2, (2 * H, D), dtype=jnp.float32) * 0.02
        w_proj = jax.random.normal(k3, (D, H), dtype=jnp.float32) * 0.02
        return {'x': x, 'w_gate_up': w_gate_up, 'w_proj': w_proj}
    _L0_ffn_all = _L0_ffn_setup()
    _L0_ffn_in = {k: v for k, v in _L0_ffn_all.items() if k in ('w_gate_up', 'w_proj')}
    del _L0_ffn_all
    return {'x': x, 'ctx_2048': ctx_2048, 'mask_BxS2_bf1': mask_BxS2_bf1, 'L0_xattn_Wq': _L0_xattn_in['Wq'], 'L0_xattn_Wk': _L0_xattn_in['Wk'], 'L0_xattn_Wv': _L0_xattn_in['Wv'], 'L0_xattn_Wo': _L0_xattn_in['Wo'], 'L0_ffn_w_gate_up': _L0_ffn_in['w_gate_up'], 'L0_ffn_w_proj': _L0_ffn_in['w_proj']}

def reference(x, ctx_2048, mask_BxS2_bf1, L0_xattn_Wq, L0_xattn_Wk, L0_xattn_Wv, L0_xattn_Wo, L0_ffn_w_gate_up, L0_ffn_w_proj):
    import jax
    import jax.numpy as jnp

    def _L0_xattn_ref(query, key, value, mask, Wq, Wk, Wv, Wo):
        import jax, jax.numpy as jnp
        import numpy as np
        import math
        D_MODEL = 512
        N_Q_HEADS = 16
        N_KV_HEADS = 4
        HEAD_DIM = D_MODEL // N_Q_HEADS
        B = 4
        S = 256

        def _alibi_slopes(num_heads):
            n = 2 ** int(math.floor(math.log2(num_heads)))
            m0 = 2.0 ** (-8.0 / n)
            return m0 ** jnp.arange(1, n + 1, dtype=jnp.float32)
        b, q_len, d = query.shape
        kv_len = key.shape[1]
        G = N_KV_HEADS
        Hpg = N_Q_HEADS // G
        dh = HEAD_DIM
        Q = (query @ Wq).reshape(b, q_len, G, Hpg, dh)
        K = (key @ Wk).reshape(b, kv_len, G, dh)
        V = (value @ Wv).reshape(b, kv_len, G, dh)
        Q = Q / math.sqrt(dh)
        scores = jnp.einsum('bqghd,bkgd->bghqk', Q, K)
        rel = jnp.arange(kv_len, dtype=jnp.float32)[None, :] - jnp.arange(q_len, dtype=jnp.float32)[:, None]
        m = _alibi_slopes(N_Q_HEADS).reshape(1, G, Hpg, 1, 1)
        scores = scores + m * rel[None, None, None]
        neg = jnp.finfo(scores.dtype).min
        scores = jnp.where(mask[:, None, None, None, :], scores, neg)
        w = jax.nn.softmax(scores, axis=-1)
        out = jnp.einsum('bghqk,bkgd->bqghd', w, V)
        out = out.reshape(b, q_len, G * Hpg * dh)
        return out @ Wo

    def _L0_ffn_ref(x, w_gate_up, w_proj):
        import jax, jax.numpy as jnp
        import numpy as np
        GROUP_SIZE = 64

        def ternary_quant(w_fp32, g=GROUP_SIZE):
            w = w_fp32.astype(jnp.bfloat16)
            w_g = w.reshape(-1, g)
            scale = jnp.clip(jnp.mean(jnp.abs(w_g), axis=-1, keepdims=True), 1e-08, None)
            q = jnp.clip(jnp.round(w_g / scale), -1, 1)
            w_hat = (q * scale).reshape(w.shape)
            return w + jax.lax.stop_gradient(w_hat - w)

        def rms_norm(x):
            eps = jnp.finfo(x.dtype).eps.astype(jnp.float32)
            xf = x.astype(jnp.float32)
            inv = jax.lax.rsqrt(jnp.mean(xf * xf, axis=-1, keepdims=True) + eps)
            return (xf * inv).astype(x.dtype)
        wq_gu = ternary_quant(w_gate_up)
        gu = jnp.einsum('bsd,hd->bsh', x, wq_gu)
        gate, up = jnp.split(gu, 2, axis=-1)
        h = jax.nn.silu(gate) * up
        hn = rms_norm(h)
        wq_p = ternary_quant(w_proj)
        return jnp.einsum('bsh,dh->bsd', hn, wq_p)
    x = x + _L0_xattn_ref(_layernorm(x, axis=-1), ctx_2048, ctx_2048, mask_BxS2_bf1, L0_xattn_Wq, L0_xattn_Wk, L0_xattn_Wv, L0_xattn_Wo)
    x = x + _L0_ffn_ref(_layernorm(x, axis=-1), L0_ffn_w_gate_up, L0_ffn_w_proj)
    return x

_drawn_inputs = setup_inputs


def setup_inputs(seed=0):
    import zlib

    import numpy as np

    out = dict(_drawn_inputs(seed))
    spreads = {}
    factors = {}
    for name, (base, spread) in spreads.items():
        noise = np.random.default_rng([zlib.crc32(name.encode()), seed]).standard_normal(out[name].shape)
        drawn = base * np.exp(spread * noise) if base else spread * noise
        out[name] = jnp.asarray(drawn.astype(out[name].dtype))
    for name, factor in factors.items():
        out[name] = (out[name] * factor).astype(out[name].dtype)
    return out
```

```python
from contextlib import ExitStack

import concourse.bass as bass
import numpy as np
from concourse import mybir

F32 = mybir.dt.float32
F16 = mybir.dt.float16
BF16 = mybir.dt.bfloat16
U8 = mybir.dt.uint8
ALU = mybir.AluOpType
ACT = mybir.ActivationFunctionType
AX = mybir.AxisListType

P = 128
B, SQ, D = 16, 100, 512
SK = 361
G, HPG, DH = 4, 4, 32
NH = G * HPG
HID = 2048
TOK = B * SQ
KC = D // P
KT = -(-SK // P)
SKP = KT * P
NM = HID // P
CH = 512
CHUNKS = [min(CH, TOK - c * CH) for c in range(-(-TOK // CH))]
TILES = [[min(P, n - i * P) for i in range(-(-n // P))] for n in CHUNKS]
UNIT = 1024
NU_GU, NU = NM, NM + NM * D // UNIT
NC = len(CHUNKS)
NT = sum(len(t) for t in TILES)
FIRST = [sum(len(t) for t in TILES[:c]) for c in range(NC)]
SEGMENTS = [[(0, 8, 2)], [(0, 3, 18), (3, 8, None)], [(0, 8, None)], [(0, 8, None)]]

WS = 64.0
ZS = 256.0
LN_EPS = 1e-5
RMS_EPS = float(np.finfo(np.float32).eps)
PSHIFT = float(10 * np.log(2))
SCORE_SCALE = 1.0 / float(np.sqrt(DH))
SCALE_MIN = 9.9837779998779297e-09
MASK_Q, MASK_K = 2048.0, 65504.0
ROW_AUX, ROW_MAX = 96, 126


def count(per, pair, parity, extra):
    return pair * (2 * per) + (per * parity + extra)


def xattn_ffn(nc, x, ctxT, mask, wq, wk, wv, wo, w_gu, w_p, qaux, kaux, kpos, ident_h,
              block_h, ones_h, out):
    with ExitStack() as ctx:
        def sb(name, shape, dt):
            return ctx.enter_context(nc.sbuf_tensor(name, shape, dt))

        def sem(name):
            return ctx.enter_context(nc.semaphore(name))

        q_dram = nc.dram_tensor("q_dram", (2, HPG, P, TOK), F16, kind="Internal").ap()
        k_dram = nc.dram_tensor("k_dram", (2, 2, P, SKP), F16, kind="Internal").ap()
        kvar_dram = nc.dram_tensor("kvar_dram", (B, 3, SKP), F16, kind="Internal").ap()
        any_dram = nc.dram_tensor("any_dram", (B, 1), F32, kind="Internal").ap()

        ident = sb("ident", [P, P], F32)
        block64 = sb("block64", [P, P], F16)
        onesf = sb("onesf", [P, P], F32)
        key_ones = sb("key_ones", [P, 2, DH], F16)
        flag = sb("flag", [P, B], F32)
        minus_half = sb("minus_half", [P, 1], F32)
        oT = sb("oT", [P, 2, HPG, TOK], F16)
        wo_s = sb("wo_s", [P, 2, KC, D], F16)
        xs = sb("xs", [P, 2, 4, D], F32)
        zT = sb("zT", [P, 2, KC, CH], F16)
        zrow = sb("zrow", [P, 2, D], F32)
        stats = sb("stats", [P, 2, 6], F32)
        mv = sb("mv", [P, 2, 2], F32)
        ve = sb("ve", [P, 2, 1], F32)
        rstd = sb("rstd", [P, 2, 1], F32)

        def carve(name, words):
            tile, at = sb(name, [P, words], F32), [0]

            def part(n):
                at[0] += n
                assert at[0] <= words
                return tile[:, at[0] - n:at[0]]
            return tile, part, at

        one, part, _ = carve("one", 2 * NM * CH)
        p32 = part(KT * G * 400).rearrange("p (t g c) -> p t g c", t=KT, g=G)
        ph = part(KT * G * 200).bitcast(F16).rearrange("p (t g c) -> p t g c", t=KT, g=G)
        pl = part(KT * G * 200).bitcast(F16).rearrange("p (t g c) -> p t g c", t=KT, g=G)
        ctx32 = part(2 * KC * SKP).rearrange("p (b k s) -> p b k s", b=2, k=KC)
        ctxs = part(2 * KC * SKP).bitcast(F16).rearrange("p (b h k s) -> p b h k s", b=2, h=2, k=KC)
        h32 = one[:, 0:NM * CH].rearrange("p (m n) -> p m n", m=NM)
        hn = one[:, NM * CH:2 * NM * CH].bitcast(F16).rearrange("p (h m n) -> p h m n", h=2, m=NM)
        w32 = [one[:, 0:2048].rearrange("p (k n) -> p k n", k=KC),
               one[:, 2048:2560].rearrange("p (k n) -> p k n", k=KC),
               one[:, 2560:3072].rearrange("p (k n) -> p k n", k=KC),
               one[:, 3072:5120].rearrange("p (k n) -> p k n", k=KC)]
        maskf = one[0:B, 5120:5120 + SK]
        maskb = one[0:B, 5504:5504 + SK]
        kvar = one[0:B, 5888:5888 + 3 * SKP // 2].bitcast(F16).rearrange("p (r s) -> p r s", r=3)
        kposs = one[0:B, 6528:6528 + SKP // 2].bitcast(F16)
        mask8 = one[0:B, 6784:6784 + 96].bitcast(U8)[:, 0:SK]

        two, part, _ = carve("two", NU * UNIT // 2)
        w_ffn = two[:, :].bitcast(BF16).rearrange("p (u n) -> p u n", u=NU)
        wq_s = part(KC * D).bitcast(F16).rearrange("p (h k n) -> p h k n", h=2, k=KC)
        wkv_s = part(KC * 2 * P).bitcast(F16).rearrange("p (h v k n) -> p h v k n", h=2, v=2, k=KC)
        kst = part(G * SKP).bitcast(F16).rearrange("p (b g s) -> p b g s", b=2, g=G)
        qst = part(NH * SQ).bitcast(F16).rearrange("p (b n q) -> p b n q", b=2, n=NH)
        vs = part(2 * KT * P).bitcast(F16).rearrange("p (b h t n) -> p b h t n", b=2, h=2, t=KT)
        qstage = part(HPG * CH).bitcast(F16).rearrange("p (h a n) -> p h a n", h=2, a=HPG)
        kh_s = part(SKP).bitcast(F16).rearrange("p (h s) -> p h s", h=2)
        rsum = part(400)
        o32 = part(400)

        wraw = sb("wraw", [P, 2, UNIT], F32)
        wtmp = sb("wtmp", [P, 4, UNIT], BF16)
        wb, wa2, wsg, wsc = (wtmp[:, i, :] for i in range(4))
        mx = sb("mx", [P, NH], F32)
        mc = sb("mc", [NH, SQ], F32)
        mrow = sb("mrow", [NH, 2, SQ], F16)
        anyk = sb("anyk", [B, 2], F32)
        sil = sb("sil", [P, 2, CH], F32)
        sqb = sb("sqb", [P, 2, CH], F32)
        acc = sb("acc", [P, CH], F32)
        rinv = sb("rinv", [P, CH], F32)

        psW = ctx.enter_context(nc.psum_tensor("psW", [P, 2, 2, 512], F32))
        psB = ctx.enter_context(nc.psum_tensor("psB", [P, 2, 512], F32))
        psO = ctx.enter_context(nc.psum_tensor("psO", [P, 2, 512], F32))

        const_ld, flag_w, flag_ld, any_done, kvar_done = (
            sem(n) for n in "const_ld flag_w flag_ld any_done kvar_done".split())
        mask_ld, mask_f, mask_b, w_ld, w_hi, w_lo, set_done = (
            sem(n) for n in "mask_ld mask_f mask_b w_ld w_hi w_lo set_done".split())
        stats_done, aggr_done, eps_added, rstd_done, z_done, zt_ps, zh_done, zl_done = (
            sem(n) for n in "stats_done aggr_done eps_added rstd_done z_done zt_ps zh_done zl_done".split())
        q_ps, qh_done, ql_done, q_wr, wo_ps, x1_done = (
            sem(n) for n in "q_ps qh_done ql_done q_wr wo_ps x1_done".split())
        ctxh_done, ctxl_done, k_ps, kh_done, kl_done, v_ps, vh_done, vl_done, k_wr = (
            sem(n) for n in "ctxh_done ctxl_done k_ps kh_done kl_done v_ps vh_done vl_done k_wr".split())
        a_ps, max_done, mt_ps, mc_done, mh_done, ml_done, b_ps, exp_done = (
            sem(n) for n in "a_ps max_done mt_ps mc_done mh_done ml_done b_ps exp_done".split())
        ph_v, ph_a, pl_p, pl_v, pv_done, rs_done, o_done, oh_done, ol_done = (
            sem(n) for n in "ph_v ph_a pl_p pl_v pv_done rs_done o_done oh_done ol_done".split())
        wb_done, wa_done, wg_done, quant_ps, scale_done, mk_done, sw_done, wh_done, wd_done, w_ready = (
            sem(n) for n in ("wb_done wa_done wg_done quant_ps scale_done mk_done sw_done wh_done "
                             "wd_done w_ready").split())
        gu_ps, sil_done, h_done, sq_done, acc_zero, acc_done, rms_ps, rt_done, sqrt_done, rinv_done = (
            sem(n) for n in ("gu_ps sil_done h_done sq_done acc_zero acc_done rms_ps rt_done "
                             "sqrt_done rinv_done").split())
        n_done, nh_done, nl_done, proj_ps, y_done = (
            sem(n) for n in "n_done nh_done nl_done proj_ps y_done".split())
        x_ld = [sem(f"x_ld{i}") for i in range(8)]
        y_st = [sem(f"y_st{i}") for i in range(8)]
        ctx_ld = [sem(f"ctx_ld{i}") for i in range(2)]
        k_rd = [sem(f"k_rd{i}") for i in range(2)]
        q_rd = [sem(f"q_rd{i}") for i in range(2)]
        m_rd = [sem(f"m_rd{i}") for i in range(2)]
        raw_ld = [sem(f"raw_ld{i}") for i in range(2)]

        x_rows = x.rearrange("b q d -> (b q) d")
        out_rows = out.rearrange("b q d -> (b q) d")

        def tile_list(c):
            return [(FIRST[c] + i, i, n) for i, n in enumerate(TILES[c])]

        def x_loads(rnd, c, i):
            before = sum(1 for r in range(2) for cc in range(NC) if (r, cc) < (rnd, c)
                         and cc % 2 == c % 2 and i < len(TILES[cc]))
            return 16 * (before + 1)

        def pipeline(fori, step):
            for j in (-2, -1, 0, 1):
                step(*(known(j + d) for d in range(4)))
            with fori(1, B // 2 - 2) as pair:
                for parity in range(2):
                    step(*((pair + (parity + d) // 2, (parity + d) % 2, 2) for d in range(4)))
            for j in range(B - 4, B):
                step(*(known(j + d) for d in range(4)))

        def known(b):
            return (b // 2, b % 2, b) if 0 <= b < B else None

        def hidden(fori, c, body):
            for lo, hi, unit in SEGMENTS[c]:
                if lo == 0 and c == 0:
                    body(0, None if unit is None else unit, True)
                    lo = 1
                with fori(lo, hi) as i:
                    body(2 * i, None if unit is None else unit + 2 * i, False)

        block = ctx.enter_context(nc.Block())

        @block.sync
        def _(sp):
            def wait(*waits):
                waits = [(s, v if isinstance(v, int) else sp.snap(sp.to_reg(v))) for s, v in waits]
                for s, v in waits:
                    sp.wait_ge(s, v)

            def load_x(rnd, c):
                for T, i, n in tile_list(c):
                    sl = (c % 2) * 4 + i
                    if rnd == 0 and c >= 2:
                        sp.wait_ge(z_done, FIRST[c - 2] + i + 1)
                    if rnd == 1 and c < 2:
                        sp.wait_ge(z_done, NT)
                    if rnd == 1 and c >= 2:
                        sp.wait_ge(y_st[sl], 16)
                    sp.dma_start(xs[0:n, c % 2, i, :], x_rows[T * P:T * P + n, :]).then_inc(x_ld[sl], 16)

            load_x(0, 0)
            sp.dma_start(ident[:, :], ident_h).then_inc(const_ld, 16)
            sp.dma_start(w32[0], wq).then_inc(w_ld, 16)
            sp.dma_start(mask8, mask).then_inc(mask_ld, 16)
            sp.dma_start(kposs, kpos).then_inc(mask_ld, 16)
            load_x(0, 1)
            for b in range(2):
                sp.dma_start(kst[ROW_AUX:P, b, :, :], kaux).then_inc(const_ld, 16)
                sp.dma_start(qst[ROW_AUX:P, b, :, :], qaux).then_inc(const_ld, 16)
            sp.dma_start(block64[:, :], block_h).then_inc(const_ld, 16)
            sp.dma_start(key_ones[:, :, :], ones_h).then_inc(const_ld, 16)
            sp.wait_ge(any_done, 2)
            sp.dma_start(any_dram, anyk[:, 1:2]).then_inc(flag_w, 16)
            sp.wait_ge(kvar_done, 4)
            sp.dma_start(kvar_dram, kvar).then_inc(flag_w, 16)
            sp.wait_ge(flag_w, 32)
            sp.dma_start(flag[:, :], any_dram.rearrange("b a -> a b").to_broadcast([P, B])
                         ).then_inc(flag_ld, 16)
            for i, w in ((1, wk), (2, wv), (3, wo)):
                sp.wait_ge(w_ld, 16 * i)
                sp.dma_start(w32[i], w).then_inc(w_ld, 16)
            sp.wait_ge(set_done, 4)

            def load_ctx(st):
                pair, par, b = st
                if b >= 2:
                    wait((ctxh_done, count(1, pair, par, -1)),
                         (ctxl_done, count(1, pair, par, -1)))
                sp.dma_start(ctx32[:, par, :, 0:SK], ctxT[2 * pair + par]).then_inc(ctx_ld[par], 16)

            load_ctx(known(0))
            load_ctx(known(1))

            for c, n in enumerate(CHUNKS):
                for half in range(2):
                    sp.wait_ge((qh_done, ql_done)[half], HPG * (c + 1))
                    sp.dma_start(q_dram[half, :, :, c * CH:c * CH + n].rearrange("a p t -> p a t"),
                                 qstage[:, half, :, 0:n]).then_inc(q_wr, 16)
                if c + 2 < NC:
                    load_x(0, c + 2)
            sp.wait_ge(q_wr, 32 * NC)

            def stack_k(st):
                pair, par, b = st
                for half in range(2):
                    wait(((kh_done, kl_done)[half], count(1, pair, par, 1)))
                    sp.dma_start(k_dram[par, half], kh_s[:, half, :]).then_inc(k_wr, 16)
                wait((k_wr, count(32, pair, par, 32)),
                     *([(b_ps, count(12, pair, par, -12))] if b >= 2 else []))
                for r, half in enumerate((0, 0, 1)):
                    sp.dma_start(kst[r * DH:(r + 1) * DH, par, :, :],
                                 k_dram[par, half].rearrange("(g d) s -> d g s", g=G)
                                 ).then_inc(k_rd[par], 16)
                for g in range(G):
                    sp.dma_start(kst[ROW_AUX:ROW_AUX + 3, par, g, :],
                                 kvar_dram[2 * pair + par]).then_inc(k_rd[par], 16)

            def stack_q(st):
                pair, par, b = st
                for r, half in enumerate((0, 1, 0)):
                    sp.dma_start(qst[r * DH:(r + 1) * DH, par, :, :],
                                 q_dram[half].rearrange("a (g d) t -> d (a g) t", g=G)
                                 [:, :, bass.ds((2 * pair + par) * SQ, SQ)]).then_inc(q_rd[par], 16)

            def max_rows(st):
                pair, par, b = st
                for half in range(2):
                    wait(((mh_done, ml_done)[half], count(1, pair, par, 1)))
                    sp.dma_start(qst[ROW_MAX + half:ROW_MAX + half + 1, par, :, :],
                                 mrow[:, half, :]).then_inc(m_rd[par], 16)

            def step(s3, s2, s1, s0):
                if s0 and s0[2] >= 2:
                    load_ctx(s0)
                if s1:
                    stack_k(s1)
                    stack_q(s1)
                if s2:
                    max_rows(s2)

            pipeline(sp.Fori, step)

            def fetch(unit, par, src, base, first):
                if not first:
                    wait((wb_done, unit - 1), (wa_done, unit - 1), (wg_done, unit - 1))
                sp.dma_start(wraw[:, par, :], src[unit - base]).then_inc(raw_ld[par], 16)

            load_x(1, 0)
            load_x(1, 1)
            for par in range(2):
                fetch(par, par, w_gu, 0, True)
            with sp.Fori(1, NU_GU // 2) as i:
                for par in range(2):
                    fetch(i * 2 + par, par, w_gu, 0, False)
            with sp.Fori(NU_GU // 2, NU // 2) as i:
                for par in range(2):
                    fetch(i * 2 + par, par, w_p, NU_GU, False)
            for c in range(NC):
                for T, i, n in tile_list(c):
                    sl = (c % 2) * 4 + i
                    sp.wait_ge(y_done, T + 1)
                    sp.dma_start(out_rows[T * P:T * P + n, :], xs[0:n, c % 2, i, :]).then_inc(y_st[sl], 16)
                if c + 2 < NC:
                    load_x(1, c + 2)
            for sl in range(8):
                sp.wait_ge(y_st[sl], 16 * sum(1 for c in range(NC) if c % 2 == sl // 4
                                              and sl % 4 < len(TILES[c])))

        @block.gpsimd
        def _(pool):
            nc.gpsimd.memset(minus_half[:, :], -0.5).then_inc(set_done, 1)
            nc.gpsimd.memset(onesf[:, :], 1.0).then_inc(set_done, 1)
            for b in range(2):
                nc.gpsimd.memset(ctx32[:, b, :, SK:SKP], 0.0).then_inc(set_done, 1)
            pool.wait_ge(set_done, 4)

            def rstd_of(k, n):
                pool.wait_ge(aggr_done, k + 1)
                if k >= 2:
                    pool.wait_ge(z_done, k - 1)
                nc.gpsimd.tensor_scalar(ve[0:n, k % 2, :], mv[0:n, k % 2, 1:2], 1.0, LN_EPS,
                                        ALU.mult, ALU.add).then_inc(eps_added, 1)
                pool.wait_ge(eps_added, k + 1)
                nc.gpsimd.tensor_tensor(rstd[0:n, k % 2, :], ve[0:n, k % 2, :], minus_half[0:n, :],
                                        ALU.pow).then_inc(rstd_done, 1)

            for c in range(NC):
                for T, i, n in tile_list(c):
                    rstd_of(T, n)

            def ctx_low(st):
                pair, par, b = st
                pool.wait_ge(ctxh_done, count(1, pair, par, 1))
                if b >= 2:
                    pool.wait_ge(v_ps, count(1, pair, par, -1))
                nc.gpsimd.tensor_tensor(ctxs[:, par, 1, :, :], ctx32[:, par, :, :], ctxs[:, par, 0, :, :],
                                        ALU.subtract).then_inc(ctxl_done, 1)

            def p_low(st, t):
                pair, par, b = st
                pool.wait_ge(ph_v, count(2, pair, par, t + 1))
                if b >= 1:
                    pool.wait_ge(pv_done, count(3, pair, par, t - 2))
                nc.gpsimd.tensor_tensor(pl[:, t, :, :], p32[:, t, :, :], ph[:, t, :, :],
                                        ALU.subtract).then_inc(pl_p, 1)

            def step(s3, s2, s1, s0):
                if s1 and s1[2] == 0:
                    ctx_low(s1)
                if s3:
                    p_low(s3, 0)
                    p_low(s3, 1)
                if s0:
                    ctx_low(s0)

            pipeline(pool.Fori, step)

            for c, n in enumerate(CHUNKS):
                for T, i, rows in tile_list(c):
                    rstd_of(NT + T, rows)
                if c:
                    pool.wait_ge(rms_ps, c)
                nc.gpsimd.memset(acc[:, :], 0.0).then_inc(acc_zero, 1)
                pool.wait_ge(acc_zero, c + 1)

                def add_squares(m0, quant, first):
                    for par in range(2):
                        pool.wait_ge(sq_done, m0 + (NM * c + par + 1))
                        if not (first and par == 0):
                            pool.wait_ge(acc_done, m0 + (NM * c + par))
                        nc.gpsimd.tensor_tensor(acc[:, 0:n], acc[:, 0:n], sqb[:, par, 0:n], ALU.add
                                                ).then_inc(acc_done, 1)

                hidden(pool.Fori, c, add_squares)

        @block.scalar
        def _(act):
            def fixed(v):
                return v if isinstance(v, int) else act.snap(act.to_reg(v))

            def z_high(k, bank, i, n, scale):
                act.wait_ge(zt_ps, k + 1)
                nc.scalar.activation(zT[:, 0, :, i * P:i * P + n],
                                     psO[:, bank, :].rearrange("p (k t) -> p k t", k=KC)[:, :, 0:n],
                                     ACT.Copy, scale=scale).then_inc(zh_done, 1)

            w_high = (wq_s[:, 0, :, :], wkv_s[:, 0, 0, :, :], wkv_s[:, 0, 1, :, :], wo_s[:, 0, :, :])
            act.wait_ge(w_ld, 16)
            nc.scalar.activation(w_high[0], w32[0], ACT.Copy, scale=WS).then_inc(w_hi, 1)
            for c, cols in enumerate(CHUNKS):
                for T, i, n in tile_list(c):
                    if i == 0 and c:
                        act.wait_ge(q_ps, HPG * c)
                    z_high(T, T % 2, i, n, 1.0)
                if c == 0:
                    for i in range(1, 4):
                        act.wait_ge(w_ld, 16 * (i + 1))
                        nc.scalar.activation(w_high[i], w32[i], ACT.Copy, scale=WS).then_inc(w_hi, 1)
                if c:
                    act.wait_ge(q_wr, 32 * c)
                for hh in range(HPG):
                    act.wait_ge(q_ps, HPG * c + hh + 1)
                    nc.scalar.activation(qstage[:, 0, hh, 0:cols], psW[:, hh // 2, hh % 2, 0:cols],
                                         ACT.Copy, scale=SCORE_SCALE / WS).then_inc(qh_done, 1)

            def ctx_high(st):
                pair, par, b = st
                act.wait_ge(ctx_ld[par], pair * 16 + 16)
                if b >= 2:
                    act.wait_ge(v_ps, count(1, pair, par, -1))
                    act.wait_ge(ctxl_done, count(1, pair, par, -1))
                nc.scalar.activation(ctxs[:, par, 0, :, :], ctx32[:, par, :, :], ACT.Copy).then_inc(ctxh_done, 1)

            def k_high(st):
                pair, par, b = st
                act.wait_ge(k_ps, count(1, pair, par, 1))
                if b >= 1:
                    act.wait_ge(k_wr, count(32, pair, par, 0))
                else:
                    act.wait_ge(flag_ld, 16)
                nc.scalar.activation(kh_s[:, 0, :], psW[:, 1, 0, 0:SKP], ACT.Copy,
                                     scale=flag[:, bass.ds(fixed(2 * pair + par), 1)]).then_inc(kh_done, 1)

            def v_high(st):
                pair, par, b = st
                act.wait_ge(v_ps, count(1, pair, par, 1))
                if b >= 2:
                    act.wait_ge(pv_done, count(3, pair, par, -3))
                nc.scalar.activation(vs[:, par, 0, :, :],
                                     psW[:, 1, 0, 0:SKP].rearrange("p (t n) -> p t n", t=KT),
                                     ACT.Copy, scale=1.0 / WS).then_inc(vh_done, 1)

            def exp(st, t, g):
                pair, par, b = st
                n = 4 * t + g
                act.wait_ge(b_ps, count(12, pair, par, n + 1))
                if b == 0 and n == 0:
                    act.wait_ge(w_hi, 4)
                    act.wait_ge(w_lo, 4)
                    act.wait_ge(flag_w, 32)
                if b >= 1 and g == 0:
                    if t < 2:
                        act.wait_ge(pl_p, count(2, pair, par, t - 1))
                    else:
                        act.wait_ge(pl_v, count(1, pair, par, 0))
                nc.scalar.activation(p32[:, t, g, :], psB[:, n % 2, 0:400], ACT.Exp).then_inc(exp_done, 1)

            def p_high(st, t):
                pair, par, b = st
                act.wait_ge(exp_done, count(12, pair, par, 4 * t + 4))
                if b >= 1:
                    act.wait_ge(pv_done, count(3, pair, par, t - 2))
                    act.wait_ge(pl_v, count(1, pair, par, 0))
                nc.scalar.activation(ph[:, t, :, :], p32[:, t, :, :], ACT.Copy).then_inc(ph_a, 1)

            def o_high(st):
                pair, par, b = st
                act.wait_ge(o_done, count(1, pair, par, 1))
                nc.scalar.activation(oT[:, 0, :, bass.ds(fixed((2 * pair + par) * SQ), SQ)],
                                     o32.rearrange("p (a q) -> p a q", a=HPG), ACT.Copy).then_inc(oh_done, 1)

            def step(s3, s2, s1, s0):
                if s1 and s1[2] == 0:
                    ctx_high(s1)
                if s1:
                    k_high(s1)
                if s3:
                    for g in range(G):
                        exp(s3, 0, g)
                if s0:
                    ctx_high(s0)
                if s3:
                    for t in (1, 2):
                        for g in range(G):
                            exp(s3, t, g)
                    p_high(s3, 2)
                if s1:
                    v_high(s1)
                if s3:
                    o_high(s3)

            pipeline(act.Fori, step)

            def quant(unit, par):
                act.wait_ge(raw_ld[par], (unit - par) * 8 + 16)
                if not isinstance(unit, int) or unit:
                    act.wait_ge(w_ready, unit)
                nc.scalar.activation(wa2, wraw[:, par, :], ACT.Abs, scale=2.0).then_inc(wa_done, 1)
                nc.scalar.activation(wb, wraw[:, par, :], ACT.Copy).then_inc(wb_done, 1)
                nc.scalar.activation(wsg, wraw[:, par, :], ACT.Sign).then_inc(wg_done, 1)

            def norm_high(c, m, par):
                act.wait_ge(n_done, m + (NM * c + 1))
                m = fixed(m)
                nc.scalar.activation(hn[:, 0, m, 0:CHUNKS[c]], h32[:, m, 0:CHUNKS[c]], ACT.Copy
                                     ).then_inc(nh_done, 1)

            def hn_free(c):
                act.wait_ge(proj_ps, FIRST[c] + len(TILES[c]))

            def root(c):
                act.wait_ge(rt_done, c + 1)
                nc.scalar.activation(rinv[:, 0:CHUNKS[c]], rinv[:, 0:CHUNKS[c]], ACT.Sqrt
                                     ).then_inc(sqrt_done, 1)

            quant(0, 0)
            quant(1, 1)
            for c, n in enumerate(CHUNKS):
                if c:
                    act.wait_ge(gu_ps, NM * c)
                for T, i, rows in tile_list(c):
                    z_high(NT + T, 1, i, rows, ZS)
                if c:
                    root(c - 1)
                if c >= 2:
                    hn_free(c - 2)

                def body(m0, unit, first):
                    for par in range(2):
                        if c:
                            norm_high(c - 1, m0 + par, par)
                        if unit is not None:
                            quant(unit + par, par)
                        act.wait_ge(gu_ps, m0 + (NM * c + par + 1))
                        if not first:
                            act.wait_ge(h_done, m0 + (NM * c + par - 1))
                        nc.scalar.activation(sil[:, par, 0:n], psW[:, par, 0, 0:n], ACT.Silu,
                                             scale=1.0 / ZS).then_inc(sil_done, 1)
                    for par in range(2):
                        act.wait_ge(h_done, m0 + (NM * c + par + 1))
                        if not first:
                            act.wait_ge(acc_done, m0 + (NM * c + par - 1))
                        nc.scalar.activation(sqb[:, par, 0:n], h32[:, fixed(m0 + par), 0:n], ACT.Square
                                             ).then_inc(sq_done, 1)

                hidden(act.Fori, c, body)
            root(NC - 1)
            hn_free(NC - 2)
            with act.Fori(0, NM) as m:
                norm_high(NC - 1, m, 0)

        @block.vector
        def _(dve):
            V = nc.vector

            def normalise(k, c, i, n, second):
                if second:
                    dve.wait_ge(x1_done, k - NT + 1)
                else:
                    dve.wait_ge(x_ld[(c % 2) * 4 + i], x_loads(0, c, i))
                if k >= 2:
                    dve.wait_ge(rstd_done, k - 1)
                    dve.wait_ge(z_done, k - 1)
                V.bn_stats(stats[0:n, k % 2, :], xs[0:n, c % 2, i, :]).then_inc(stats_done, 1)
                dve.wait_ge(stats_done, k + 1)
                V.bn_aggr(mv[0:n, k % 2, :], stats[0:n, k % 2, :]).then_inc(aggr_done, 1)

            def z_of(k, c, i, n):
                dve.wait_ge(rstd_done, k + 1)
                if k >= 2:
                    dve.wait_ge(zt_ps, k - 1)
                V.tensor_scalar(zrow[0:n, k % 2, :], xs[0:n, c % 2, i, :], mv[0:n, k % 2, 0:1],
                                rstd[0:n, k % 2, :], ALU.subtract, ALU.mult).then_inc(z_done, 1)

            def z_low(k, bank, i, n, scale):
                dve.wait_ge(zh_done, k + 1)
                V.scalar_tensor_tensor(out=zT[:, 1, :, i * P:i * P + n],
                                       in0=psO[:, bank, :].rearrange("p (k t) -> p k t", k=KC)[:, :, 0:n],
                                       scalar=scale, in1=zT[:, 0, :, i * P:i * P + n],
                                       op0=ALU.mult, op1=ALU.subtract).then_inc(zl_done, 1)

            w_low = (wq_s[:, :, :, :], wkv_s[:, :, 0, :, :], wkv_s[:, :, 1, :, :], wo_s[:, :, :, :])

            def split_w(i):
                dve.wait_ge(w_hi, i + 1)
                V.scalar_tensor_tensor(out=w_low[i][:, 1, :, :], in0=w32[i], scalar=WS,
                                       in1=w_low[i][:, 0, :, :], op0=ALU.mult, op1=ALU.subtract
                                       ).then_inc(w_lo, 1)

            def masks():
                V.memset(kvar, 0.0).then_inc(kvar_done, 1)
                dve.wait_ge(mask_ld, 32)
                V.tensor_copy(maskf, mask8).then_inc(mask_f, 1)
                dve.wait_ge(mask_f, 1)
                V.tensor_reduce(anyk[:, 0:1], maskf, AX.X, ALU.max).then_inc(any_done, 1)
                V.tensor_scalar(maskb, maskf, 1.0, MASK_K, ALU.subtract, ALU.mult).then_inc(mask_b, 1)
                dve.wait_ge(any_done, 1)
                V.tensor_scalar(anyk[:, 1:2], anyk[:, 0:1], 1.0 / WS, None, ALU.mult).then_inc(any_done, 1)
                dve.wait_ge(kvar_done, 1)
                for r in range(2):
                    V.tensor_scalar(kvar[:, r, :], kposs, anyk[:, 0:1], None, ALU.mult).then_inc(kvar_done, 1)
                dve.wait_ge(mask_b, 1)
                V.tensor_scalar(kvar[:, 2, 0:SK], maskb, anyk[:, 0:1], None, ALU.mult).then_inc(kvar_done, 1)

            for c, cols in enumerate(CHUNKS):
                if c:
                    dve.wait_ge(q_ps, HPG * c)
                for T, i, n in tile_list(c):
                    normalise(T, c, i, n, False)
                    z_of(T, c, i, n)
                    if i:
                        z_low(T - 1, (T - 1) % 2, i - 1, P, 1.0)
                z_low(T, T % 2, i, n, 1.0)
                if c == 0:
                    split_w(0)
                    masks()
                    for i in range(1, 4):
                        split_w(i)
                if c:
                    dve.wait_ge(q_wr, 32 * c)
                for hh in range(HPG):
                    dve.wait_ge(qh_done, HPG * c + hh + 1)
                    V.scalar_tensor_tensor(out=qstage[:, 1, hh, 0:cols], in0=psW[:, hh // 2, hh % 2, 0:cols],
                                           scalar=SCORE_SCALE / WS, in1=qstage[:, 0, hh, 0:cols],
                                           op0=ALU.mult, op1=ALU.subtract).then_inc(ql_done, 1)

            def k_low(st):
                pair, par, b = st
                dve.wait_ge(kh_done, count(1, pair, par, 1))
                if b >= 1:
                    dve.wait_ge(k_wr, count(32, pair, par, 0))
                V.scalar_tensor_tensor(out=kh_s[:, 1, :], in0=psW[:, 1, 0, 0:SKP],
                                       scalar=flag[:, bass.ds(2 * pair + par, 1)], in1=kh_s[:, 0, :],
                                       op0=ALU.mult, op1=ALU.subtract).then_inc(kl_done, 1)

            def v_low(st):
                pair, par, b = st
                dve.wait_ge(vh_done, count(1, pair, par, 1))
                V.scalar_tensor_tensor(out=vs[:, par, 1, :, :],
                                       in0=psW[:, 1, 0, 0:SKP].rearrange("p (t n) -> p t n", t=KT),
                                       scalar=1.0 / WS, in1=vs[:, par, 0, :, :],
                                       op0=ALU.mult, op1=ALU.subtract).then_inc(vl_done, 1)

            def maxima(st, u):
                pair, par, b = st
                dve.wait_ge(a_ps, count(8, pair, par, u + 1))
                if b >= 1 and u == 0:
                    dve.wait_ge(mt_ps, count(1, pair, par, 0))
                V.tensor_reduce(mx[0:SQ, 2 * u:2 * u + 2], psW[0:SQ, u % 2, :, 0:SK], AX.X, ALU.max,
                                negate=True).then_inc(max_done, 1)

            def max_split(st):
                pair, par, b = st
                dve.wait_ge(mt_ps, count(1, pair, par, 1))
                if b >= 1:
                    before = pair if par else pair - 1
                    dve.wait_ge(ml_done, count(1, pair, par, 0))
                    dve.wait_ge(m_rd[1 - par], before * 32 + 32)
                V.tensor_scalar(mc[:, :], psW[0:NH, 0, 0, 0:SQ], PSHIFT, None, ALU.add).then_inc(mc_done, 1)
                dve.wait_ge(mc_done, count(1, pair, par, 1))
                V.tensor_copy(mrow[:, 0, :], mc[:, :]).then_inc(mh_done, 1)
                dve.wait_ge(mh_done, count(1, pair, par, 1))
                V.tensor_tensor(mrow[:, 1, :], mc[:, :], mrow[:, 0, :], ALU.subtract).then_inc(ml_done, 1)

            def p_high(st, t):
                pair, par, b = st
                dve.wait_ge(exp_done, count(12, pair, par, 4 * t + 4))
                if b >= 1:
                    dve.wait_ge(pv_done, count(3, pair, par, t - 2))
                V.tensor_copy(ph[:, t, :, :], p32[:, t, :, :]).then_inc(ph_v, 1)

            def p_low(st, t):
                pair, par, b = st
                dve.wait_ge(ph_a, count(1, pair, par, 1))
                if b >= 1:
                    dve.wait_ge(pv_done, count(3, pair, par, t - 2))
                V.tensor_tensor(pl[:, t, :, :], p32[:, t, :, :], ph[:, t, :, :], ALU.subtract).then_inc(pl_v, 1)

            def attended(st):
                pair, par, b = st
                dve.wait_ge(pv_done, count(3, pair, par, 3))
                if b >= 1:
                    dve.wait_ge(o_done, count(1, pair, par, 0))
                V.reciprocal(rsum, psO[:, 1, 0:400]).then_inc(rs_done, 1)
                dve.wait_ge(rs_done, count(1, pair, par, 1))
                if b >= 1:
                    dve.wait_ge(oh_done, count(1, pair, par, 0))
                    dve.wait_ge(ol_done, count(1, pair, par, 0))
                V.tensor_tensor(o32, psO[:, 0, 0:400], rsum, ALU.mult).then_inc(o_done, 1)

            def o_low(st):
                pair, par, b = st
                dve.wait_ge(oh_done, count(1, pair, par, 1))
                at = bass.ds((2 * pair + par) * SQ, SQ)
                V.tensor_tensor(oT[:, 1, :, at], o32.rearrange("p (a q) -> p a q", a=HPG), oT[:, 0, :, at],
                                ALU.subtract).then_inc(ol_done, 1)

            def step(s3, s2, s1, s0):
                if s1:
                    k_low(s1)
                for u in range(8):
                    if s2:
                        maxima(s2, u)
                    if s3 and u == 2:
                        p_high(s3, 0)
                    if s3 and u == 5:
                        p_high(s3, 1)
                if s2:
                    max_split(s2)
                if s3:
                    p_low(s3, 2)
                    attended(s3)
                if s1:
                    v_low(s1)
                if s3:
                    o_low(s3)

            pipeline(dve.Fori, step)

            def quant(unit, par):
                dve.wait_ge(quant_ps, unit + 1)
                V.tensor_scalar(wsc, psB[:, :, :].rearrange("p a n -> p (a n)"), SCALE_MIN, None, ALU.max
                                ).then_inc(scale_done, 1)
                dve.wait_ge(scale_done, unit + 1)
                V.tensor_tensor(wa2, wa2, wsc, ALU.is_gt).then_inc(mk_done, 1)
                dve.wait_ge(wg_done, unit + 1)
                V.tensor_tensor(wsg, wsg, wsc, ALU.mult).then_inc(sw_done, 1)
                dve.wait_ge(mk_done, unit + 1)
                dve.wait_ge(sw_done, unit + 1)
                V.tensor_tensor(wsg, wsg, wa2, ALU.mult).then_inc(wh_done, 1)
                dve.wait_ge(wh_done, unit + 1)
                V.tensor_tensor(wsg, wsg, wb, ALU.subtract).then_inc(wd_done, 1)
                dve.wait_ge(wd_done, unit + 1)
                V.tensor_tensor(w_ffn[:, unit, :], wb, wsg, ALU.add).then_inc(w_ready, 1)

            def norm(c, m):
                n = CHUNKS[c]
                V.scalar_tensor_tensor(out=h32[:, m, 0:n], in0=h32[:, m, 0:n], scalar=ZS, in1=rinv[:, 0:n],
                                       op0=ALU.mult, op1=ALU.mult).then_inc(n_done, 1)

            def norm_low(c, m):
                n = CHUNKS[c]
                dve.wait_ge(nh_done, m + (NM * c + 1))
                V.tensor_tensor(hn[:, 1, m, 0:n], h32[:, m, 0:n], hn[:, 0, m, 0:n], ALU.subtract
                                ).then_inc(nl_done, 1)

            def inverse_rms(c):
                n = CHUNKS[c]
                dve.wait_ge(rms_ps, c + 1)
                if c:
                    dve.wait_ge(n_done, NM * c)
                V.tensor_scalar(rinv[:, 0:n], psO[:, 1, 0:n], 1.0 / HID, RMS_EPS, ALU.mult, ALU.add
                                ).then_inc(rt_done, 1)
                dve.wait_ge(sqrt_done, c + 1)
                V.reciprocal(rinv[:, 0:n], rinv[:, 0:n]).then_inc(rinv_done, 1)
                dve.wait_ge(rinv_done, c + 1)
                if c:
                    dve.wait_ge(proj_ps, FIRST[c])

            def result(c):
                for T, i, n in tile_list(c):
                    dve.wait_ge(proj_ps, T + 1)
                    V.scalar_tensor_tensor(out=xs[0:n, c % 2, i, :], in0=psO[0:n, i % 2, :], scalar=1.0 / ZS,
                                           in1=xs[0:n, c % 2, i, :], op0=ALU.mult, op1=ALU.add
                                           ).then_inc(y_done, 1)

            dve.wait_ge(oh_done, B)
            dve.wait_ge(ol_done, B)
            dve.wait_ge(v_ps, B)
            quant(0, 0)
            quant(1, 1)
            for c, n in enumerate(CHUNKS):
                if c:
                    dve.wait_ge(gu_ps, NM * c)
                for T, i, rows in tile_list(c):
                    k = NT + T
                    dve.wait_ge(wo_ps, T + 1)
                    dve.wait_ge(x_ld[(c % 2) * 4 + i], x_loads(1, c, i))
                    V.scalar_tensor_tensor(out=xs[0:rows, c % 2, i, :], in0=psO[0:rows, 0, :], scalar=1.0 / WS,
                                           in1=xs[0:rows, c % 2, i, :], op0=ALU.mult, op1=ALU.add
                                           ).then_inc(x1_done, 1)
                    normalise(k, c, i, rows, True)
                    z_of(k, c, i, rows)
                    z_low(k, 1, i, rows, ZS)
                if c:
                    inverse_rms(c - 1)

                def body(m0, unit, first):
                    if c:
                        norm(c - 1, m0)
                        norm(c - 1, m0 + 1)
                    for par in range(2):
                        m = m0 + par
                        if c:
                            norm_low(c - 1, m)
                        if unit is not None:
                            quant(unit + par, par)
                        dve.wait_ge(sil_done, m0 + (NM * c + par + 1))
                        if c:
                            dve.wait_ge(nl_done, m0 + (NM * (c - 1) + par + 1))
                        V.scalar_tensor_tensor(out=h32[:, m, 0:n], in0=psW[:, par, 1, 0:n], scalar=1.0 / ZS,
                                               in1=sil[:, par, 0:n], op0=ALU.mult, op1=ALU.mult
                                               ).then_inc(h_done, 1)

                hidden(dve.Fori, c, body)
                if c:
                    result(c - 1)
            inverse_rms(NC - 1)
            with dve.Fori(0, NM) as m:
                norm(NC - 1, m)
                dve.wait_ge(n_done, m + (NM * (NC - 1) + 1))
                norm_low(NC - 1, m)
            result(NC - 1)

        @block.tensor
        def _(pe):
            def product(dst, pairs):
                for i, (left, right) in enumerate(pairs):
                    last = nc.tensor.matmul(dst, left, right, start=(i == 0), stop=(i == len(pairs) - 1))
                return last

            HALVES = ((0, 0), (0, 1), (1, 0))

            def turn(k, bank, n):
                pe.wait_ge(z_done, k + 1)
                for kk in range(KC):
                    last = nc.tensor.transpose(psO[:, bank, kk * P:kk * P + n],
                                               zrow[0:n, k % 2, kk * P:(kk + 1) * P], ident[0:n, 0:n])
                last.then_inc(zt_ps, 1)

            pe.wait_ge(const_ld, 16 * 7)
            for c, cols in enumerate(CHUNKS):
                for T, i, n in tile_list(c):
                    if T >= 2:
                        pe.wait_ge(zl_done, T - 1)
                    turn(T, T % 2, n)
                pe.wait_ge(w_lo, 1)
                pe.wait_ge(zl_done, T + 1)
                if c:
                    pe.wait_ge(ql_done, HPG * c)
                for hh in range(HPG):
                    product(psW[:, hh // 2, hh % 2, 0:cols],
                            [(wq_s[:, a, k, hh * P:(hh + 1) * P], zT[:, b, k, 0:cols])
                             for k in range(KC) for a, b in HALVES]).then_inc(q_ps, 1)

            def k_proj(st):
                pair, par, b = st
                pe.wait_ge(ctxl_done, count(1, pair, par, 1))
                if b == 0:
                    pe.wait_ge(w_lo, 3)
                    pe.wait_ge(ql_done, HPG * NC)
                else:
                    pe.wait_ge(vl_done, count(1, pair, par, 0))
                product(psW[:, 1, 0, 0:SKP],
                        [(wkv_s[:, a, 0, k, :], ctxs[:, par, h, k, :])
                         for k in range(KC) for a, h in HALVES]).then_inc(k_ps, 1)

            def v_proj(st):
                pair, par, b = st
                pe.wait_ge(kl_done, count(1, pair, par, 1))
                if b >= 1:
                    pe.wait_ge(max_done, count(8, pair, par, 0))
                for t in range(KT):
                    last = product(psW[:, 1, 0, t * P:(t + 1) * P],
                                   [(ctxs[:, par, h, k, t * P:(t + 1) * P], wkv_s[:, a, 1, k, :])
                                    for k in range(KC) for a, h in HALVES])
                last.then_inc(v_ps, 1)

            def score_rows(st, u):
                pair, par, b = st
                if u == 0:
                    pe.wait_ge(k_rd[par], pair * 112 + 112)
                    pe.wait_ge(q_rd[par], pair * 48 + 48)
                    if b >= 1:
                        pe.wait_ge(mc_done, count(1, pair, par, 0))
                elif u == 1:
                    if b < B - 1:
                        pe.wait_ge(kl_done, count(1, pair, par, 2))
                    else:
                        pe.wait_ge(vl_done, B)
                else:
                    pe.wait_ge(max_done, count(8, pair, par, u - 1))
                for e in range(2):
                    n = 2 * u + e
                    last = nc.tensor.matmul(psW[0:SQ, u % 2, e, 0:SK], qst[0:ROW_MAX, par, n, :],
                                            kst[0:ROW_MAX, par, n % G, 0:SK], start=True, stop=True)
                last.then_inc(a_ps, 1)

            def max_turn(st):
                pair, par, b = st
                pe.wait_ge(max_done, count(8, pair, par, 8))
                nc.tensor.transpose(psW[0:NH, 0, 0, 0:SQ], mx[0:SQ, :], ident[0:SQ, 0:SQ]).then_inc(mt_ps, 1)

            def score_cols(st, n):
                pair, par, b = st
                t, g = n // G, n % G
                if n == 0:
                    pe.wait_ge(m_rd[par], pair * 32 + 32)
                if n >= 2 or b >= 1:
                    pe.wait_ge(exp_done, count(12, pair, par, n - 1))
                nc.tensor.matmul(psB[:, n % 2, 0:400], kst[:, par, g, t * P:(t + 1) * P],
                                 qst[:, par, :, :].rearrange("p (a g) q -> p a g q", g=G)[:, :, g, :],
                                 start=True, stop=True).then_inc(b_ps, 1)

            def attend(st, t):
                pair, par, b = st
                if t == 0:
                    pe.wait_ge(vl_done, count(1, pair, par, 1))
                    if b >= 1:
                        pe.wait_ge(o_done, count(1, pair, par, 0))
                if t < 2:
                    pe.wait_ge(pl_p, count(2, pair, par, t + 1))
                else:
                    pe.wait_ge(pl_v, count(1, pair, par, 1))
                ones = key_ones[:, 1 if t == KT - 1 else 0, :]
                for bank, half, probs in ((0, 0, ph), (0, 0, pl), (0, 1, ph), (1, None, ph), (1, None, pl)):
                    for g in range(G):
                        left = ones if half is None else vs[:, par, half, t, g * DH:(g + 1) * DH]
                        last = nc.tensor.matmul(
                            psO[g * DH:(g + 1) * DH, bank, 0:400], left, probs[:, t, g, :],
                            start=(t == 0 and probs is ph and half != 1),
                            stop=(t == KT - 1 and (half == 1 or (half is None and probs is pl))))
                last.then_inc(pv_done, 1)

            def step(s3, s2, s1, s0):
                if s1:
                    k_proj(s1)
                order = "B B A B A B A B A B A B A B 0 A B A B T B B 1 2".split()
                n = u = 0
                for what in order:
                    if what == "B":
                        if s3:
                            score_cols(s3, n)
                        n += 1
                    elif what == "A":
                        if s2:
                            score_rows(s2, u)
                        u += 1
                    elif what == "T":
                        if s2:
                            max_turn(s2)
                    elif s3:
                        attend(s3, int(what))
                if s1:
                    v_proj(s1)

            pipeline(pe.Fori, step)

            def project(T, c, i, n):
                pe.wait_ge(w_lo, 4)
                if T:
                    pe.wait_ge(x1_done, T)
                if T == 0:
                    pe.wait_ge(ol_done, B)
                if c >= 2:
                    pe.wait_ge(y_done, FIRST[c - 1])
                at = c * CH + i * P
                product(psO[0:n, 0, :], [(oT[:, a, k, at:at + n], wo_s[:, b, k, :])
                                         for k in range(KC) for a, b in HALVES]).then_inc(wo_ps, 1)

            def scales(unit, par):
                pe.wait_ge(wa_done, unit + 1)
                if isinstance(unit, int) and unit == 0:
                    pe.wait_ge(exp_done, 12 * B)
                else:
                    pe.wait_ge(scale_done, unit)
                for e in range(2):
                    last = nc.tensor.matmul(psB[:, e, :], block64[:, :], wa2[:, e * 512:(e + 1) * 512],
                                            start=True, stop=True)
                last.then_inc(quant_ps, 1)

            def square_sums(c):
                pe.wait_ge(acc_done, NM * (c + 1))
                if c == NC - 1:
                    pe.wait_ge(y_done, FIRST[c])
                pe.wait_ge(zl_done, NT + FIRST[min(c + 1, NC - 1)] + len(TILES[min(c + 1, NC - 1)]))
                nc.tensor.matmul(psO[:, 1, 0:CHUNKS[c]], onesf[:, :], acc[:, 0:CHUNKS[c]],
                                 start=True, stop=True).then_inc(rms_ps, 1)

            def down(c):
                pe.wait_ge(w_ready, NU)
                pe.wait_ge(nl_done, NM * (c + 1))
                pe.wait_ge(rt_done, c + 1)
                for T, i, n in tile_list(c):
                    if i < 2:
                        pe.wait_ge(x1_done, FIRST[min(c + 1, NC - 1)] + len(TILES[min(c + 1, NC - 1)]))
                        if T:
                            pe.wait_ge(y_done, T if i == 0 else T - 1)
                    else:
                        pe.wait_ge(y_done, T - 1)
                    product(psO[0:n, i % 2, :],
                            [(hn[:, h, m, i * P:i * P + n], w_ffn[:, NU_GU + m // 2, (m % 2) * D:(m % 2 + 1) * D])
                             for m in range(NM) for h in range(2)]).then_inc(proj_ps, 1)

            scales(0, 0)
            scales(1, 1)
            for c, n in enumerate(CHUNKS):
                tiles = tile_list(c)
                project(*tiles[0][:1], c, *tiles[0][1:])
                for e, (T, i, rows) in enumerate(tiles):
                    if e + 1 < len(tiles):
                        T1, i1, rows1 = tiles[e + 1]
                        project(T1, c, i1, rows1)
                    if T:
                        pe.wait_ge(zl_done, NT + T)
                    if c:
                        pe.wait_ge(y_done, FIRST[c - 1])
                        if c >= 2:
                            pe.wait_ge(rt_done, c - 1)
                    turn(NT + T, 1, rows)
                if c:
                    square_sums(c - 1)
                pe.wait_ge(zl_done, NT + FIRST[c] + len(tiles))

                def body(m0, unit, first):
                    for par in range(2):
                        if unit is not None:
                            scales(unit + par, par)
                        M = m0 + (NM * c + par)
                        if not first:
                            pe.wait_ge(h_done, M - 1)
                        if c == 0:
                            pe.wait_ge(w_ready, m0 + (par + 1))
                        for e in range(2):
                            last = product(psW[:, par, e, 0:n],
                                           [(w_ffn[:, m0 + par, k * 256 + e * P:k * 256 + (e + 1) * P],
                                             zT[:, h, k, 0:n]) for k in range(KC) for h in range(2)])
                        last.then_inc(gu_ps, 1)

                hidden(pe.Fori, c, body)
                if c:
                    down(c - 1)
            square_sums(NC - 1)
            down(NC - 1)


_OUTS = [((B, SQ, D), "float32")]


def constants():
    f16 = np.float16
    slope = np.float32(2.0 ** (-8.0 / NH)) ** np.arange(1, NH + 1, dtype=np.float32)
    order = [g * HPG + a for a in range(HPG) for g in range(G)]
    slope = slope[order].astype(np.float64)
    qaux = np.zeros((P - ROW_AUX, NH, SQ), f16)
    off = -slope[:, None] * np.arange(SQ)[None, :]
    for row, v in ((0, np.repeat(slope[:, None], SQ, 1)), (3, off)):
        hi = v.astype(f16)
        lo = (v - hi.astype(np.float64)).astype(f16)
        if row == 0:
            qaux[0], qaux[1] = hi, lo
        else:
            qaux[3], qaux[4] = hi, lo
    qaux[2] = MASK_Q
    kaux = np.zeros((P - ROW_AUX, G, SKP), f16)
    for row in (3, 4, ROW_MAX - ROW_AUX, ROW_MAX - ROW_AUX + 1):
        kaux[row, :, :SK] = 1.0
    kpos = np.zeros((B, SKP), f16)
    kpos[:, :SK] = np.arange(SK)
    key_ones = np.ones((P, 2, DH), f16)
    key_ones[SK - (KT - 1) * P:, 1] = 0.0
    block = np.kron(np.eye(2), np.full((64, 64), 2.0 ** -7)).astype(f16)
    return {"qaux": qaux, "kaux": kaux, "kpos": kpos, "ident": np.eye(P, dtype=np.float32),
            "block64": block, "key_ones": key_ones}


def layouts(x, ctx_2048, mask_BxS2_bf1, L0_xattn_Wq, L0_xattn_Wk, L0_xattn_Wv, L0_xattn_Wo,
            L0_ffn_w_gate_up, L0_ffn_w_proj):
    def rows(w):
        return w.reshape(KC, P, -1).transpose(1, 0, 2)

    wq = L0_xattn_Wq.reshape(KC, P, G, HPG, DH).transpose(1, 0, 3, 2, 4).reshape(P, KC, D)
    wo = L0_xattn_Wo.reshape(G, HPG, DH, D).transpose(0, 2, 1, 3).reshape(P, HPG, D)
    gu = L0_ffn_w_gate_up.reshape(2, NM, P, KC, P).transpose(1, 4, 3, 0, 2).reshape(NM, P, UNIT)
    p = L0_ffn_w_proj.reshape(D, NM // 2, 2, P).transpose(1, 3, 2, 0).reshape(NM // 2, P, UNIT)
    return {"x": x, "ctxT": ctx_2048.reshape(B, SK, KC, P).transpose(0, 3, 2, 1),
            "mask": mask_BxS2_bf1.view(np.uint8), "wq": wq, "wk": rows(L0_xattn_Wk),
            "wv": rows(L0_xattn_Wv), "wo": wo, "w_gu": gu, "w_p": p}


def kernel(**inputs):
    import concourse.bacc as _bacc
    from concourse.bass_utils import run_bass_kernel_spmd as _run

    nc = _bacc.Bacc("TRN2", target_bir_lowering=False, num_devices=1)
    arrays, args = {}, []
    for name, a in {**layouts(**{k: np.asarray(v) for k, v in inputs.items()}), **constants()}.items():
        a = np.ascontiguousarray(a)
        arrays[f"in_{name}"] = a
        args.append(nc.dram_tensor(f"in_{name}", a.shape, mybir.dt.from_np(a.dtype), kind="ExternalInput").ap())
    for i, (shape, dtype) in enumerate(_OUTS):
        args.append(nc.dram_tensor(f"out_{i}", shape, mybir.dt.from_np(np.dtype(dtype)), kind="ExternalOutput").ap())
    xattn_ffn(nc, *args)
    r = _run(nc, [arrays], core_ids=[0])
    return r.results[0]["out_0"]
```

```python
from contextlib import ExitStack

import concourse.bass as bass
import numpy as np
from concourse import mybir

F32 = mybir.dt.float32
F16 = mybir.dt.float16
BF16 = mybir.dt.bfloat16
U8 = mybir.dt.uint8
ALU = mybir.AluOpType
ACT = mybir.ActivationFunctionType
AX = mybir.AxisListType

P = 128
B, SQ, D = 16, 100, 512
SK = 361
G, HPG, DH = 4, 4, 32
NH = G * HPG
HID = 2048
TOK = B * SQ
KC = D // P
KT = -(-SK // P)
SKP = KT * P
NM = HID // P
CH = 512
CHUNKS = [min(CH, TOK - c * CH) for c in range(-(-TOK // CH))]
TILES = [[min(P, n - i * P) for i in range(-(-n // P))] for n in CHUNKS]
UNIT = 1024
NU_GU, NU = NM, NM + NM * D // UNIT
NC = len(CHUNKS)
SLOT = (0, 0, 1, 0, 1, 0, 1, 0)
NT = sum(len(t) for t in TILES)
FIRST = [sum(len(t) for t in TILES[:c]) for c in range(NC)]
SEGMENTS = [[(0, 8, 2)], [(0, 3, 18), (3, 8, None)], [(0, 8, None)], [(0, 8, None)]]

WS = 64.0
ZS = 256.0
LN_EPS = 1e-5
RMS_EPS = float(np.finfo(np.float32).eps)
PSHIFT = float(10 * np.log(2))
SCORE_SCALE = 1.0 / float(np.sqrt(DH))
SCALE_MIN = 9.9837779998779297e-09
MASK_Q, MASK_K = 2048.0, 65504.0
ROW_AUX, ROW_MAX = 96, 126


def count(per, pair, parity, extra):
    return pair * (2 * per) + (per * parity + extra)


def xattn_ffn(nc, x, ctxT, mask, wq, wk, wv, wo, w_gu, w_p, qaux, kaux, kpos, ident_h,
              block_h, ones_h, out):
    with ExitStack() as ctx:
        def sb(name, shape, dt):
            return ctx.enter_context(nc.sbuf_tensor(name, shape, dt))

        def sem(name):
            return ctx.enter_context(nc.semaphore(name))

        q_dram = nc.dram_tensor("q_dram", (3 * DH, HPG, G, TOK), F16, kind="Internal").ap()
        k_dram = nc.dram_tensor("k_dram", (B, 3 * DH + 3, G, SKP), F16, kind="Internal").ap()
        any_dram = nc.dram_tensor("any_dram", (B, 1), F32, kind="Internal").ap()

        ident = sb("ident", [P, P], F32)
        block64 = sb("block64", [P, P], F16)
        onesf = sb("onesf", [P, P], F32)
        key_ones = sb("key_ones", [P, 2, DH], F16)
        flag = sb("flag", [P, B], F32)
        minus_half = sb("minus_half", [P, 1], F32)
        oT = sb("oT", [P, 2, HPG, TOK], F16)
        wo_s = sb("wo_s", [P, 2, KC, D], F16)
        xs = sb("xs", [P, 2, 4, D], F32)
        zT = sb("zT", [P, 2, KC, CH], F16)
        zrow = sb("zrow", [P, 2, D], F32)
        stats = sb("stats", [P, 2, 6], F32)
        mv = sb("mv", [P, 2, 2], F32)
        ve = sb("ve", [P, 2, 1], F32)
        rstd = sb("rstd", [P, 2, 1], F32)

        def carve(name, words):
            tile, at = sb(name, [P, words], F32), [0]

            def part(n):
                at[0] += n
                assert at[0] <= words
                return tile[:, at[0] - n:at[0]]
            return tile, part, at

        one, part, _ = carve("one", 2 * NM * CH)
        p32 = part(KT * G * 400).rearrange("p (t g c) -> p t g c", t=KT, g=G)
        ph = part(KT * G * 200).bitcast(F16).rearrange("p (t g c) -> p t g c", t=KT, g=G)
        pl = part(KT * G * 200).bitcast(F16).rearrange("p (t g c) -> p t g c", t=KT, g=G)
        ctx32 = part(2 * KC * SKP).rearrange("p (b k s) -> p b k s", b=2, k=KC)
        ctxs = part(2 * KC * SKP).bitcast(F16).rearrange("p (b h k s) -> p b h k s", b=2, h=2, k=KC)
        h32 = one[:, 0:NM * CH].rearrange("p (m n) -> p m n", m=NM)
        hn = one[:, NM * CH:2 * NM * CH].bitcast(F16).rearrange("p (h m n) -> p h m n", h=2, m=NM)
        w32 = [one[:, 0:2048].rearrange("p (k n) -> p k n", k=KC),
               one[:, 2048:2560].rearrange("p (k n) -> p k n", k=KC),
               one[:, 2560:3072].rearrange("p (k n) -> p k n", k=KC),
               one[:, 3072:5120].rearrange("p (k n) -> p k n", k=KC)]
        maskf = one[0:B, 5120:5120 + SK]
        maskb = one[0:B, 5504:5504 + SK]
        kvar = one[0:B, 5888:5888 + 3 * SKP // 2].bitcast(F16).rearrange("p (r s) -> p r s", r=3)
        kposs = one[0:B, 6528:6528 + SKP // 2].bitcast(F16)
        mask8 = one[0:B, 6784:6784 + 96].bitcast(U8)[:, 0:SK]

        two, part, _ = carve("two", NU * UNIT // 2)
        w_ffn = two[:, :].bitcast(BF16).rearrange("p (u n) -> p u n", u=NU)
        wq_s = part(KC * D).bitcast(F16).rearrange("p (h k n) -> p h k n", h=2, k=KC)
        wkv_s = part(KC * 2 * P).bitcast(F16).rearrange("p (h v k n) -> p h v k n", h=2, v=2, k=KC)
        kst = part(G * SKP).bitcast(F16).rearrange("p (b g s) -> p b g s", b=2, g=G)
        qst = part(NH * SQ).bitcast(F16).rearrange("p (b n q) -> p b n q", b=2, n=NH)
        vs = part(2 * KT * P).bitcast(F16).rearrange("p (b h t n) -> p b h t n", b=2, h=2, t=KT)
        qstage = part(HPG * CH).bitcast(F16).rearrange("p (h a n) -> p h a n", h=2, a=HPG)
        kh_s = part(SKP).bitcast(F16).rearrange("p (h s) -> p h s", h=2)
        rsum = part(400)
        o32 = part(400)

        wraw = sb("wraw", [P, 2, UNIT], F32)
        wtmp = sb("wtmp", [P, 4, UNIT], BF16)
        wb, wa2, wsg, wsc = (wtmp[:, i, :] for i in range(4))
        mx = sb("mx", [P, NH], F32)
        mc = sb("mc", [NH, SQ], F32)
        mrow = sb("mrow", [NH, 2, SQ], F16)
        anyk = sb("anyk", [B, 2], F32)
        sil = sb("sil", [P, 2, CH], F32)
        sqb = sb("sqb", [P, 2, CH], F32)
        acc = sb("acc", [P, CH], F32)
        rinv = sb("rinv", [P, CH], F32)

        psW = ctx.enter_context(nc.psum_tensor("psW", [P, 2, 2, 512], F32))
        psB = ctx.enter_context(nc.psum_tensor("psB", [P, 2, 512], F32))
        psO = ctx.enter_context(nc.psum_tensor("psO", [P, 2, 512], F32))

        const_ld, flag_w, flag_ld, any_done, kvar_done = (
            sem(n) for n in "const_ld flag_w flag_ld any_done kvar_done".split())
        mask_ld, mask_f, mask_b, w_ld, w_hi, w_lo, set_done = (
            sem(n) for n in "mask_ld mask_f mask_b w_ld w_hi w_lo set_done".split())
        stats_done, aggr_done, eps_added, rstd_done, z_done, zt_ps, zh_done, zl_done = (
            sem(n) for n in "stats_done aggr_done eps_added rstd_done z_done zt_ps zh_done zl_done".split())
        q_ps, qh_done, ql_done, q_wr, wo_ps, x1_done = (
            sem(n) for n in "q_ps qh_done ql_done q_wr wo_ps x1_done".split())
        ctxh_done, ctxl_done, k_ps, kh_done, kl_done, v_ps, vh_done, vl_done, k_wr = (
            sem(n) for n in "ctxh_done ctxl_done k_ps kh_done kl_done v_ps vh_done vl_done k_wr".split())
        a_ps, max_done, mt_ps, mc_done, mh_done, ml_done, b_ps, exp_done = (
            sem(n) for n in "a_ps max_done mt_ps mc_done mh_done ml_done b_ps exp_done".split())
        ph_v, ph_a, pl_p, pl_v, pv_done, rs_done, o_done, oh_done, ol_done = (
            sem(n) for n in "ph_v ph_a pl_p pl_v pv_done rs_done o_done oh_done ol_done".split())
        wb_done, wa_done, wg_done, quant_ps, scale_done, mk_done, sw_done, wh_done, wd_done, w_ready = (
            sem(n) for n in ("wb_done wa_done wg_done quant_ps scale_done mk_done sw_done wh_done "
                             "wd_done w_ready").split())
        gu_ps, sil_done, h_done, sq_done, acc_zero, acc_done, rms_ps, rt_done, sqrt_done, rinv_done = (
            sem(n) for n in ("gu_ps sil_done h_done sq_done acc_zero acc_done rms_ps rt_done "
                             "sqrt_done rinv_done").split())
        n_done, nh_done, nl_done, proj_ps, y_done = (
            sem(n) for n in "n_done nh_done nl_done proj_ps y_done".split())
        x_ld = [sem(f"x_ld{i}") for i in range(8)]
        y_st = [sem(f"y_st{i}") for i in range(8)]
        ctx_ld = [sem(f"ctx_ld{i}") for i in range(2)]
        k_rd = [sem(f"k_rd{i}") for i in range(2)]
        q_rd = [sem(f"q_rd{i}") for i in range(2)]
        m_rd = [sem(f"m_rd{i}") for i in range(2)]
        raw_ld = [sem(f"raw_ld{i}") for i in range(2)]

        x_rows = x.rearrange("b q d -> (b q) d")
        out_rows = out.rearrange("b q d -> (b q) d")

        def tile_list(c):
            return [(FIRST[c] + i, i, n) for i, n in enumerate(TILES[c])]

        def x_loads(rnd, c, i):
            before = sum(1 for r in range(2) for cc in range(NC) if (r, cc) < (rnd, c)
                         and cc % 2 == c % 2 and i < len(TILES[cc]))
            return 16 * (before + 1)

        def pipeline(fori, step):
            for j in (-3, -2, -1, 0, 1):
                step(*(known(j + d) for d in range(-1, 4)))
            with fori(1, B // 2 - 2) as pair:
                for parity in range(2):
                    step(*((pair + (parity + d) // 2, (parity + d) % 2, 2) for d in range(-1, 4)))
            for j in range(B - 4, B + 1):
                step(*(known(j + d) for d in range(-1, 4)))

        def known(b):
            return (b // 2, b % 2, b) if 0 <= b < B else None

        def hidden(fori, c, body):
            for lo, hi, unit in SEGMENTS[c]:
                if lo == 0 and c == 0:
                    body(0, None if unit is None else unit, True)
                    lo = 1
                with fori(lo, hi) as i:
                    body(2 * i, None if unit is None else unit + 2 * i, False)

        block = ctx.enter_context(nc.Block())

        @block.sync
        def _(sp):
            def wait(*waits):
                waits = [(s, v if isinstance(v, int) else sp.snap(sp.to_reg(v))) for s, v in waits]
                for s, v in waits:
                    sp.wait_ge(s, v)

            def load_x(rnd, c):
                for T, i, n in tile_list(c):
                    sl = (c % 2) * 4 + i
                    if rnd == 0 and c >= 2:
                        sp.wait_ge(z_done, FIRST[c - 2] + i + 1)
                    if rnd == 1 and c < 2:
                        sp.wait_ge(z_done, NT)
                    if rnd == 1 and c >= 2:
                        sp.wait_ge(y_st[sl], 16)
                    sp.dma_start(xs[0:n, c % 2, i, :], x_rows[T * P:T * P + n, :]).then_inc(x_ld[sl], 16)

            load_x(0, 0)
            sp.dma_start(ident[:, :], ident_h).then_inc(const_ld, 16)
            sp.dma_start(w32[0], wq).then_inc(w_ld, 16)
            sp.dma_start(mask8, mask).then_inc(mask_ld, 16)
            sp.dma_start(kposs, kpos).then_inc(mask_ld, 16)
            load_x(0, 1)
            for b in range(2):
                sp.dma_start(kst[ROW_AUX:P, b, :, :], kaux).then_inc(const_ld, 16)
                sp.dma_start(qst[ROW_AUX:P, b, :, :], qaux).then_inc(const_ld, 16)
            sp.dma_start(block64[:, :], block_h).then_inc(const_ld, 16)
            sp.dma_start(key_ones[:, :, :], ones_h).then_inc(const_ld, 16)
            sp.wait_ge(any_done, 2)
            sp.dma_start(any_dram, anyk[:, 1:2]).then_inc(flag_w, 16)
            sp.wait_ge(kvar_done, 4)
            for g in range(G):
                sp.dma_start(k_dram[:, 3 * DH:, g, :], kvar).then_inc(flag_w, 16)
            sp.wait_ge(flag_w, 16 * (G + 1))
            sp.dma_start(flag[:, :], any_dram.rearrange("b a -> a b").to_broadcast([P, B])
                         ).then_inc(flag_ld, 16)
            for i, w in ((1, wk), (2, wv), (3, wo)):
                sp.wait_ge(w_ld, 16 * i)
                sp.dma_start(w32[i], w).then_inc(w_ld, 16)
            sp.wait_ge(set_done, 4)

            def load_ctx(st):
                pair, par, b = st
                if b >= 2:
                    wait((ctxh_done, count(1, pair, par, -1)),
                         (ctxl_done, count(1, pair, par, -1)))
                sp.dma_start(ctx32[:, par, :, 0:SK], ctxT[2 * pair + par]).then_inc(ctx_ld[par], 16)

            load_ctx(known(0))
            load_ctx(known(1))

            for c, n in enumerate(CHUNKS):
                for r, half in ((0, 0), (2, 0), (1, 1)):
                    sp.wait_ge((qh_done, ql_done)[half], HPG * (c + 1))
                    for g in range(G):
                        sp.dma_start(q_dram[r * DH:(r + 1) * DH, :, g, c * CH:c * CH + n],
                                     qstage[g * DH:(g + 1) * DH, half, :, 0:n]).then_inc(q_wr, 16)
                if c + 2 < NC:
                    load_x(0, c + 2)
            sp.wait_ge(q_wr, 48 * G * NC)

            def write_k(st):
                pair, par, b = st
                for r, half in ((0, 0), (1, 0), (2, 1)):
                    wait(((kh_done, kl_done)[half], count(1, pair, par, 1)))
                    sp.dma_start(k_dram[2 * pair + par, r * DH:(r + 1) * DH].rearrange("d g s -> g d s"),
                                 kh_s[:, half, :]).then_inc(k_wr, 16)

            def fill_stacks(st):
                pair, par, b = st
                wait((k_wr, count(48, pair, par, 48)),
                     *([(b_ps, count(12, pair, par, -12))] if b >= 2 else []))
                sp.dma_start(kst[0:3 * DH + 3, par, :, :], k_dram[2 * pair + par]).then_inc(k_rd[par], 16)
                sp.dma_start(qst[0:3 * DH, par, :, :], q_dram[:, :, :, bass.ds((2 * pair + par) * SQ, SQ)]
                             .rearrange("p a g t -> p (a g) t")).then_inc(q_rd[par], 16)

            def step(m1, s0, p1, p2, p3):
                if p3 and p3[2] >= 2:
                    load_ctx(p3)
                if p2:
                    write_k(p2)
                    fill_stacks(p2)

            pipeline(sp.Fori, step)

            def fetch(unit, par, src, base, first):
                if not first:
                    wait((wb_done, unit - 1), (wa_done, unit - 1), (wg_done, unit - 1))
                sp.dma_start(wraw[:, par, :], src[unit - base]).then_inc(raw_ld[par], 16)

            load_x(1, 0)
            load_x(1, 1)
            for par in range(2):
                fetch(par, par, w_gu, 0, True)
            with sp.Fori(1, NU_GU // 2) as i:
                for par in range(2):
                    fetch(i * 2 + par, par, w_gu, 0, False)
            with sp.Fori(NU_GU // 2, NU // 2) as i:
                for par in range(2):
                    fetch(i * 2 + par, par, w_p, NU_GU, False)
            for c in range(NC):
                for T, i, n in tile_list(c):
                    sl = (c % 2) * 4 + i
                    sp.wait_ge(y_done, T + 1)
                    sp.dma_start(out_rows[T * P:T * P + n, :], xs[0:n, c % 2, i, :]).then_inc(y_st[sl], 16)
                if c + 2 < NC:
                    load_x(1, c + 2)
            for sl in range(8):
                sp.wait_ge(y_st[sl], 16 * sum(1 for c in range(NC) if c % 2 == sl // 4
                                              and sl % 4 < len(TILES[c])))

        @block.gpsimd
        def _(pool):
            nc.gpsimd.memset(minus_half[:, :], -0.5).then_inc(set_done, 1)
            nc.gpsimd.memset(onesf[:, :], 1.0).then_inc(set_done, 1)
            for b in range(2):
                nc.gpsimd.memset(ctx32[:, b, :, SK:SKP], 0.0).then_inc(set_done, 1)
            pool.wait_ge(set_done, 4)

            def rstd_of(k, n):
                pool.wait_ge(aggr_done, k + 1)
                if k >= 2:
                    pool.wait_ge(z_done, k - 1)
                nc.gpsimd.tensor_scalar(ve[0:n, k % 2, :], mv[0:n, k % 2, 1:2], 1.0, LN_EPS,
                                        ALU.mult, ALU.add).then_inc(eps_added, 1)
                pool.wait_ge(eps_added, k + 1)
                nc.gpsimd.tensor_tensor(rstd[0:n, k % 2, :], ve[0:n, k % 2, :], minus_half[0:n, :],
                                        ALU.pow).then_inc(rstd_done, 1)

            for c in range(NC):
                for T, i, n in tile_list(c):
                    rstd_of(T, n)

            def ctx_low(st):
                pair, par, b = st
                pool.wait_ge(ctxh_done, count(1, pair, par, 1))
                if b >= 2:
                    pool.wait_ge(v_ps, count(1, pair, par, -1))
                nc.gpsimd.tensor_tensor(ctxs[:, par, 1, :, :], ctx32[:, par, :, :], ctxs[:, par, 0, :, :],
                                        ALU.subtract).then_inc(ctxl_done, 1)

            def p_low(st, t):
                pair, par, b = st
                if t == 0:
                    pool.wait_ge(ph_v, count(1, pair, par, 1))
                else:
                    pool.wait_ge(ph_a, count(2, pair, par, 1))
                if b >= 1:
                    pool.wait_ge(pv_done, count(3, pair, par, t - 2))
                nc.gpsimd.tensor_tensor(pl[:, t, :, :], p32[:, t, :, :], ph[:, t, :, :],
                                        ALU.subtract).then_inc(pl_p, 1)

            def step(m1, s0, p1, p2, p3):
                if s0:
                    p_low(s0, 0)
                if p3:
                    ctx_low(p3)
                if s0:
                    p_low(s0, 1)

            pipeline(pool.Fori, step)

            for c, n in enumerate(CHUNKS):
                for T, i, rows in tile_list(c):
                    rstd_of(NT + T, rows)
                if c:
                    pool.wait_ge(rms_ps, c)
                nc.gpsimd.memset(acc[:, :], 0.0).then_inc(acc_zero, 1)
                pool.wait_ge(acc_zero, c + 1)

                def add_squares(m0, quant, first):
                    for par in range(2):
                        pool.wait_ge(sq_done, m0 + (NM * c + par + 1))
                        if not (first and par == 0):
                            pool.wait_ge(acc_done, m0 + (NM * c + par))
                        nc.gpsimd.tensor_tensor(acc[:, 0:n], acc[:, 0:n], sqb[:, par, 0:n], ALU.add
                                                ).then_inc(acc_done, 1)

                hidden(pool.Fori, c, add_squares)

        @block.scalar
        def _(act):
            def fixed(v):
                return v if isinstance(v, int) else act.snap(act.to_reg(v))

            def z_high(k, bank, i, n, scale):
                act.wait_ge(zt_ps, k + 1)
                nc.scalar.activation(zT[:, 0, :, i * P:i * P + n],
                                     psO[:, bank, :].rearrange("p (k t) -> p k t", k=KC)[:, :, 0:n],
                                     ACT.Copy, scale=scale).then_inc(zh_done, 1)

            w_high = (wq_s[:, 0, :, :], wkv_s[:, 0, 0, :, :], wkv_s[:, 0, 1, :, :], wo_s[:, 0, :, :])
            act.wait_ge(w_ld, 16)
            nc.scalar.activation(w_high[0], w32[0], ACT.Copy, scale=WS).then_inc(w_hi, 1)
            for c, cols in enumerate(CHUNKS):
                for T, i, n in tile_list(c):
                    if i == 0 and c:
                        act.wait_ge(q_ps, HPG * c)
                    z_high(T, T % 2, i, n, 1.0)
                if c == 0:
                    for i in range(1, 4):
                        act.wait_ge(w_ld, 16 * (i + 1))
                        nc.scalar.activation(w_high[i], w32[i], ACT.Copy, scale=WS).then_inc(w_hi, 1)
                if c:
                    act.wait_ge(q_wr, 48 * G * c)
                for hh in range(HPG):
                    act.wait_ge(q_ps, HPG * c + hh + 1)
                    nc.scalar.activation(qstage[:, 0, hh, 0:cols], psW[:, hh // 2, hh % 2, 0:cols],
                                         ACT.Copy, scale=SCORE_SCALE / WS).then_inc(qh_done, 1)

            def ctx_high(st):
                pair, par, b = st
                act.wait_ge(ctx_ld[par], pair * 16 + 16)
                if b >= 2:
                    act.wait_ge(v_ps, count(1, pair, par, -1))
                    act.wait_ge(ctxl_done, count(1, pair, par, -1))
                nc.scalar.activation(ctxs[:, par, 0, :, :], ctx32[:, par, :, :], ACT.Copy).then_inc(ctxh_done, 1)

            def k_high(st):
                pair, par, b = st
                act.wait_ge(k_ps, count(1, pair, par, 1))
                if b >= 1:
                    act.wait_ge(k_wr, count(48, pair, par, 0))
                else:
                    act.wait_ge(flag_ld, 16)
                nc.scalar.activation(kh_s[:, 0, :], psW[:, 1, 0, 0:SKP], ACT.Copy,
                                     scale=flag[:, bass.ds(fixed(2 * pair + par), 1)]).then_inc(kh_done, 1)

            def v_high(st):
                pair, par, b = st
                act.wait_ge(v_ps, count(1, pair, par, 1))
                if b >= 2:
                    act.wait_ge(pv_done, count(3, pair, par, -3))
                nc.scalar.activation(vs[:, par, 0, :, :],
                                     psW[:, 1, 1, 0:SKP].rearrange("p (t n) -> p t n", t=KT),
                                     ACT.Copy, scale=1.0 / WS).then_inc(vh_done, 1)

            def exp(st, t, g):
                pair, par, b = st
                n = 4 * t + g
                act.wait_ge(b_ps, count(12, pair, par, n + 1))
                if b == 0 and n == 0:
                    act.wait_ge(w_hi, 4)
                    act.wait_ge(w_lo, 4)
                    act.wait_ge(flag_w, 16 * (G + 1))
                if b >= 1 and g == 0:
                    if t < 2:
                        act.wait_ge(pl_p, count(2, pair, par, t - 1))
                    else:
                        act.wait_ge(pl_v, count(1, pair, par, 0))
                nc.scalar.activation(p32[:, t, g, :], psB[:, n % 2, 0:400], ACT.Exp).then_inc(exp_done, 1)

            def p_high(st, t):
                pair, par, b = st
                act.wait_ge(exp_done, count(12, pair, par, 4 * t + 4))
                if b >= 1:
                    act.wait_ge(pv_done, count(3, pair, par, t - 2))
                nc.scalar.activation(ph[:, t, :, :], p32[:, t, :, :], ACT.Copy).then_inc(ph_a, 1)

            def max_rows(st):
                pair, par, b = st
                for half in range(2):
                    act.wait_ge((mh_done, ml_done)[half], count(1, pair, par, 1))
                    act.dma_start(qst[ROW_MAX + half:ROW_MAX + half + 1, par, :, :],
                                  mrow[:, half, :]).then_inc(m_rd[par], 16)

            def o_high(st):
                pair, par, b = st
                act.wait_ge(o_done, count(1, pair, par, 1))
                nc.scalar.activation(oT[:, 0, :, bass.ds(fixed((2 * pair + par) * SQ), SQ)],
                                     o32.rearrange("p (a q) -> p a q", a=HPG), ACT.Copy).then_inc(oh_done, 1)

            def step(m1, s0, p1, p2, p3):
                if p2:
                    k_high(p2)
                if s0:
                    for g in range(G):
                        exp(s0, 0, g)
                if p1:
                    v_high(p1)
                if m1:
                    o_high(m1)
                if s0:
                    exp(s0, 1, 0)
                    exp(s0, 1, 1)
                if p3:
                    ctx_high(p3)
                if s0:
                    exp(s0, 1, 2)
                    exp(s0, 1, 3)
                    p_high(s0, 1)
                    for g in range(G):
                        exp(s0, 2, g)
                    p_high(s0, 2)
                if p1:
                    max_rows(p1)

            pipeline(act.Fori, step)

            def quant(unit, par):
                act.wait_ge(raw_ld[par], (unit - par) * 8 + 16)
                if not isinstance(unit, int) or unit:
                    act.wait_ge(w_ready, unit)
                nc.scalar.activation(wa2, wraw[:, par, :], ACT.Abs, scale=2.0).then_inc(wa_done, 1)
                nc.scalar.activation(wb, wraw[:, par, :], ACT.Copy).then_inc(wb_done, 1)
                nc.scalar.activation(wsg, wraw[:, par, :], ACT.Sign).then_inc(wg_done, 1)

            def norm_high(c, m, par):
                act.wait_ge(n_done, m + (NM * c + 1))
                m = fixed(m)
                nc.scalar.activation(hn[:, 0, m, 0:CHUNKS[c]], h32[:, m, 0:CHUNKS[c]], ACT.Copy
                                     ).then_inc(nh_done, 1)

            def hn_free(c):
                act.wait_ge(proj_ps, FIRST[c] + len(TILES[c]))

            def root(c):
                act.wait_ge(rt_done, c + 1)
                nc.scalar.activation(rinv[:, 0:CHUNKS[c]], rinv[:, 0:CHUNKS[c]], ACT.Sqrt
                                     ).then_inc(sqrt_done, 1)

            quant(0, 0)
            quant(1, 1)
            for c, n in enumerate(CHUNKS):
                if c:
                    act.wait_ge(gu_ps, NM * c)
                for T, i, rows in tile_list(c):
                    z_high(NT + T, 1, i, rows, ZS)
                if c:
                    root(c - 1)
                if c >= 2:
                    hn_free(c - 2)

                def body(m0, unit, first):
                    for par in range(2):
                        if c:
                            norm_high(c - 1, m0 + par, par)
                        if unit is not None:
                            quant(unit + par, par)
                        act.wait_ge(gu_ps, m0 + (NM * c + par + 1))
                        if not first:
                            act.wait_ge(h_done, m0 + (NM * c + par - 1))
                        nc.scalar.activation(sil[:, par, 0:n], psW[:, par, 0, 0:n], ACT.Silu,
                                             scale=1.0 / ZS).then_inc(sil_done, 1)
                    for par in range(2):
                        act.wait_ge(h_done, m0 + (NM * c + par + 1))
                        if not first:
                            act.wait_ge(acc_done, m0 + (NM * c + par - 1))
                        nc.scalar.activation(sqb[:, par, 0:n], h32[:, fixed(m0 + par), 0:n], ACT.Square
                                             ).then_inc(sq_done, 1)

                hidden(act.Fori, c, body)
            root(NC - 1)
            hn_free(NC - 2)
            with act.Fori(0, NM) as m:
                norm_high(NC - 1, m, 0)

        @block.vector
        def _(dve):
            V = nc.vector

            def normalise(k, c, i, n, second):
                if second:
                    dve.wait_ge(x1_done, k - NT + 1)
                else:
                    dve.wait_ge(x_ld[(c % 2) * 4 + i], x_loads(0, c, i))
                if k >= 2:
                    dve.wait_ge(rstd_done, k - 1)
                    dve.wait_ge(z_done, k - 1)
                V.bn_stats(stats[0:n, k % 2, :], xs[0:n, c % 2, i, :]).then_inc(stats_done, 1)
                dve.wait_ge(stats_done, k + 1)
                V.bn_aggr(mv[0:n, k % 2, :], stats[0:n, k % 2, :]).then_inc(aggr_done, 1)

            def z_of(k, c, i, n):
                dve.wait_ge(rstd_done, k + 1)
                if k >= 2:
                    dve.wait_ge(zt_ps, k - 1)
                V.tensor_scalar(zrow[0:n, k % 2, :], xs[0:n, c % 2, i, :], mv[0:n, k % 2, 0:1],
                                rstd[0:n, k % 2, :], ALU.subtract, ALU.mult).then_inc(z_done, 1)

            def z_low(k, bank, i, n, scale):
                dve.wait_ge(zh_done, k + 1)
                V.scalar_tensor_tensor(out=zT[:, 1, :, i * P:i * P + n],
                                       in0=psO[:, bank, :].rearrange("p (k t) -> p k t", k=KC)[:, :, 0:n],
                                       scalar=scale, in1=zT[:, 0, :, i * P:i * P + n],
                                       op0=ALU.mult, op1=ALU.subtract).then_inc(zl_done, 1)

            w_low = (wq_s[:, :, :, :], wkv_s[:, :, 0, :, :], wkv_s[:, :, 1, :, :], wo_s[:, :, :, :])

            def split_w(i):
                dve.wait_ge(w_hi, i + 1)
                V.scalar_tensor_tensor(out=w_low[i][:, 1, :, :], in0=w32[i], scalar=WS,
                                       in1=w_low[i][:, 0, :, :], op0=ALU.mult, op1=ALU.subtract
                                       ).then_inc(w_lo, 1)

            def masks():
                V.memset(kvar, 0.0).then_inc(kvar_done, 1)
                dve.wait_ge(mask_ld, 32)
                V.tensor_copy(maskf, mask8).then_inc(mask_f, 1)
                dve.wait_ge(mask_f, 1)
                V.tensor_reduce(anyk[:, 0:1], maskf, AX.X, ALU.max).then_inc(any_done, 1)
                V.tensor_scalar(maskb, maskf, 1.0, MASK_K, ALU.subtract, ALU.mult).then_inc(mask_b, 1)
                dve.wait_ge(any_done, 1)
                V.tensor_scalar(anyk[:, 1:2], anyk[:, 0:1], 1.0 / WS, None, ALU.mult).then_inc(any_done, 1)
                dve.wait_ge(kvar_done, 1)
                for r in range(2):
                    V.tensor_scalar(kvar[:, r, :], kposs, anyk[:, 0:1], None, ALU.mult).then_inc(kvar_done, 1)
                dve.wait_ge(mask_b, 1)
                V.tensor_scalar(kvar[:, 2, 0:SK], maskb, anyk[:, 0:1], None, ALU.mult).then_inc(kvar_done, 1)

            for c, cols in enumerate(CHUNKS):
                if c:
                    dve.wait_ge(q_ps, HPG * c)
                for T, i, n in tile_list(c):
                    normalise(T, c, i, n, False)
                    z_of(T, c, i, n)
                    if i:
                        z_low(T - 1, (T - 1) % 2, i - 1, P, 1.0)
                z_low(T, T % 2, i, n, 1.0)
                if c == 0:
                    split_w(0)
                    masks()
                    for i in range(1, 4):
                        split_w(i)
                if c:
                    dve.wait_ge(q_wr, 48 * G * c)
                for hh in range(HPG):
                    dve.wait_ge(qh_done, HPG * c + hh + 1)
                    V.scalar_tensor_tensor(out=qstage[:, 1, hh, 0:cols], in0=psW[:, hh // 2, hh % 2, 0:cols],
                                           scalar=SCORE_SCALE / WS, in1=qstage[:, 0, hh, 0:cols],
                                           op0=ALU.mult, op1=ALU.subtract).then_inc(ql_done, 1)

            def k_low(st):
                pair, par, b = st
                dve.wait_ge(kh_done, count(1, pair, par, 1))
                if b >= 1:
                    dve.wait_ge(k_wr, count(48, pair, par, 0))
                V.scalar_tensor_tensor(out=kh_s[:, 1, :], in0=psW[:, 1, 0, 0:SKP],
                                       scalar=flag[:, bass.ds(2 * pair + par, 1)], in1=kh_s[:, 0, :],
                                       op0=ALU.mult, op1=ALU.subtract).then_inc(kl_done, 1)

            def v_low(st):
                pair, par, b = st
                dve.wait_ge(vh_done, count(1, pair, par, 1))
                V.scalar_tensor_tensor(out=vs[:, par, 1, :, :],
                                       in0=psW[:, 1, 1, 0:SKP].rearrange("p (t n) -> p t n", t=KT),
                                       scalar=1.0 / WS, in1=vs[:, par, 0, :, :],
                                       op0=ALU.mult, op1=ALU.subtract).then_inc(vl_done, 1)

            def maxima(st, u):
                pair, par, b = st
                dve.wait_ge(a_ps, count(8, pair, par, u + 1))
                if b >= 1 and u == 0:
                    dve.wait_ge(mt_ps, count(1, pair, par, 0))
                V.tensor_reduce(mx[0:SQ, 2 * u:2 * u + 2], psW[0:SQ, SLOT[u], :, 0:SK], AX.X, ALU.max,
                                negate=True).then_inc(max_done, 1)

            def max_split(st):
                pair, par, b = st
                dve.wait_ge(mt_ps, count(1, pair, par, 1))
                if b >= 1:
                    before = pair if par else pair - 1
                    dve.wait_ge(ml_done, count(1, pair, par, 0))
                    dve.wait_ge(m_rd[1 - par], before * 32 + 32)
                V.tensor_scalar(mc[:, :], psW[0:NH, 0, 0, 0:SQ], PSHIFT, None, ALU.add).then_inc(mc_done, 1)
                dve.wait_ge(mc_done, count(1, pair, par, 1))
                V.tensor_copy(mrow[:, 0, :], mc[:, :]).then_inc(mh_done, 1)
                dve.wait_ge(mh_done, count(1, pair, par, 1))
                V.tensor_tensor(mrow[:, 1, :], mc[:, :], mrow[:, 0, :], ALU.subtract).then_inc(ml_done, 1)

            def p_high(st, t):
                pair, par, b = st
                dve.wait_ge(exp_done, count(12, pair, par, 4 * t + 4))
                if b >= 1:
                    dve.wait_ge(pv_done, count(3, pair, par, t - 2))
                V.tensor_copy(ph[:, t, :, :], p32[:, t, :, :]).then_inc(ph_v, 1)

            def p_low(st, t):
                pair, par, b = st
                dve.wait_ge(ph_a, count(2, pair, par, 2))
                if b >= 1:
                    dve.wait_ge(pv_done, count(3, pair, par, t - 2))
                V.tensor_tensor(pl[:, t, :, :], p32[:, t, :, :], ph[:, t, :, :], ALU.subtract).then_inc(pl_v, 1)

            def attended(st):
                pair, par, b = st
                dve.wait_ge(pv_done, count(3, pair, par, 3))
                if b >= 1:
                    dve.wait_ge(o_done, count(1, pair, par, 0))
                V.reciprocal(rsum, psO[:, 1, 0:400]).then_inc(rs_done, 1)
                dve.wait_ge(rs_done, count(1, pair, par, 1))
                if b >= 1:
                    dve.wait_ge(oh_done, count(1, pair, par, 0))
                    dve.wait_ge(ol_done, count(1, pair, par, 0))
                V.tensor_tensor(o32, psO[:, 0, 0:400], rsum, ALU.mult).then_inc(o_done, 1)

            def o_low(st):
                pair, par, b = st
                dve.wait_ge(oh_done, count(1, pair, par, 1))
                at = bass.ds((2 * pair + par) * SQ, SQ)
                V.tensor_tensor(oT[:, 1, :, at], o32.rearrange("p (a q) -> p a q", a=HPG), oT[:, 0, :, at],
                                ALU.subtract).then_inc(ol_done, 1)

            def step(m1, s0, p1, p2, p3):
                if m1:
                    p_low(m1, 2)
                if p2:
                    k_low(p2)
                if p1:
                    maxima(p1, 0)
                if m1:
                    attended(m1)
                if s0:
                    p_high(s0, 0)
                if p1:
                    v_low(p1)
                    maxima(p1, 1)
                    maxima(p1, 2)
                if m1:
                    o_low(m1)
                if p1:
                    for u in range(3, 8):
                        maxima(p1, u)
                    max_split(p1)

            pipeline(dve.Fori, step)

            def quant(unit, par):
                dve.wait_ge(quant_ps, unit + 1)
                V.tensor_scalar(wsc, psB[:, :, :].rearrange("p a n -> p (a n)"), SCALE_MIN, None, ALU.max
                                ).then_inc(scale_done, 1)
                dve.wait_ge(scale_done, unit + 1)
                V.tensor_tensor(wa2, wa2, wsc, ALU.is_gt).then_inc(mk_done, 1)
                dve.wait_ge(wg_done, unit + 1)
                V.tensor_tensor(wsg, wsg, wsc, ALU.mult).then_inc(sw_done, 1)
                dve.wait_ge(mk_done, unit + 1)
                dve.wait_ge(sw_done, unit + 1)
                V.tensor_tensor(wsg, wsg, wa2, ALU.mult).then_inc(wh_done, 1)
                dve.wait_ge(wh_done, unit + 1)
                V.tensor_tensor(wsg, wsg, wb, ALU.subtract).then_inc(wd_done, 1)
                dve.wait_ge(wd_done, unit + 1)
                V.tensor_tensor(w_ffn[:, unit, :], wb, wsg, ALU.add).then_inc(w_ready, 1)

            def norm(c, m):
                n = CHUNKS[c]
                V.scalar_tensor_tensor(out=h32[:, m, 0:n], in0=h32[:, m, 0:n], scalar=ZS, in1=rinv[:, 0:n],
                                       op0=ALU.mult, op1=ALU.mult).then_inc(n_done, 1)

            def norm_low(c, m):
                n = CHUNKS[c]
                dve.wait_ge(nh_done, m + (NM * c + 1))
                V.tensor_tensor(hn[:, 1, m, 0:n], h32[:, m, 0:n], hn[:, 0, m, 0:n], ALU.subtract
                                ).then_inc(nl_done, 1)

            def inverse_rms(c):
                n = CHUNKS[c]
                dve.wait_ge(rms_ps, c + 1)
                if c:
                    dve.wait_ge(n_done, NM * c)
                V.tensor_scalar(rinv[:, 0:n], psO[:, 1, 0:n], 1.0 / HID, RMS_EPS, ALU.mult, ALU.add
                                ).then_inc(rt_done, 1)
                dve.wait_ge(sqrt_done, c + 1)
                V.reciprocal(rinv[:, 0:n], rinv[:, 0:n]).then_inc(rinv_done, 1)
                dve.wait_ge(rinv_done, c + 1)
                if c:
                    dve.wait_ge(proj_ps, FIRST[c])

            def result(c):
                for T, i, n in tile_list(c):
                    dve.wait_ge(proj_ps, T + 1)
                    V.scalar_tensor_tensor(out=xs[0:n, c % 2, i, :], in0=psO[0:n, i % 2, :], scalar=1.0 / ZS,
                                           in1=xs[0:n, c % 2, i, :], op0=ALU.mult, op1=ALU.add
                                           ).then_inc(y_done, 1)

            dve.wait_ge(oh_done, B)
            dve.wait_ge(ol_done, B)
            dve.wait_ge(v_ps, B)
            quant(0, 0)
            quant(1, 1)
            for c, n in enumerate(CHUNKS):
                if c:
                    dve.wait_ge(gu_ps, NM * c)
                for T, i, rows in tile_list(c):
                    k = NT + T
                    dve.wait_ge(wo_ps, T + 1)
                    dve.wait_ge(x_ld[(c % 2) * 4 + i], x_loads(1, c, i))
                    V.scalar_tensor_tensor(out=xs[0:rows, c % 2, i, :], in0=psO[0:rows, 0, :], scalar=1.0 / WS,
                                           in1=xs[0:rows, c % 2, i, :], op0=ALU.mult, op1=ALU.add
                                           ).then_inc(x1_done, 1)
                    normalise(k, c, i, rows, True)
                    z_of(k, c, i, rows)
                    z_low(k, 1, i, rows, ZS)
                if c:
                    inverse_rms(c - 1)

                def body(m0, unit, first):
                    if c:
                        norm(c - 1, m0)
                        norm(c - 1, m0 + 1)
                    for par in range(2):
                        m = m0 + par
                        if c:
                            norm_low(c - 1, m)
                        if unit is not None:
                            quant(unit + par, par)
                        dve.wait_ge(sil_done, m0 + (NM * c + par + 1))
                        if c:
                            dve.wait_ge(nl_done, m0 + (NM * (c - 1) + par + 1))
                        V.scalar_tensor_tensor(out=h32[:, m, 0:n], in0=psW[:, par, 1, 0:n], scalar=1.0 / ZS,
                                               in1=sil[:, par, 0:n], op0=ALU.mult, op1=ALU.mult
                                               ).then_inc(h_done, 1)

                hidden(dve.Fori, c, body)
                if c:
                    result(c - 1)
            inverse_rms(NC - 1)
            with dve.Fori(0, NM) as m:
                norm(NC - 1, m)
                dve.wait_ge(n_done, m + (NM * (NC - 1) + 1))
                norm_low(NC - 1, m)
            result(NC - 1)

        @block.tensor
        def _(pe):
            def product(dst, pairs):
                for i, (left, right) in enumerate(pairs):
                    last = nc.tensor.matmul(dst, left, right, start=(i == 0), stop=(i == len(pairs) - 1))
                return last

            HALVES = ((0, 0), (0, 1), (1, 0))

            def turn(k, bank, n):
                pe.wait_ge(z_done, k + 1)
                for kk in range(KC):
                    last = nc.tensor.transpose(psO[:, bank, kk * P:kk * P + n],
                                               zrow[0:n, k % 2, kk * P:(kk + 1) * P], ident[0:n, 0:n])
                last.then_inc(zt_ps, 1)

            pe.wait_ge(const_ld, 16 * 7)
            for c, cols in enumerate(CHUNKS):
                for T, i, n in tile_list(c):
                    if T >= 2:
                        pe.wait_ge(zl_done, T - 1)
                    turn(T, T % 2, n)
                pe.wait_ge(w_lo, 1)
                pe.wait_ge(zl_done, T + 1)
                if c:
                    pe.wait_ge(ql_done, HPG * c)
                for hh in range(HPG):
                    product(psW[:, hh // 2, hh % 2, 0:cols],
                            [(wq_s[:, a, k, hh * P:(hh + 1) * P], zT[:, b, k, 0:cols])
                             for k in range(KC) for a, b in HALVES]).then_inc(q_ps, 1)

            def k_proj(st):
                pair, par, b = st
                pe.wait_ge(ctxl_done, count(1, pair, par, 1))
                if b == 0:
                    pe.wait_ge(w_lo, 3)
                    pe.wait_ge(ql_done, HPG * NC)
                elif b == 1:
                    pe.wait_ge(kl_done, 1)
                else:
                    pe.wait_ge(max_done, count(8, pair, par, -9))
                product(psW[:, 1, 0, 0:SKP],
                        [(wkv_s[:, a, 0, k, :], ctxs[:, par, h, k, :])
                         for k in range(KC) for a, h in HALVES]).then_inc(k_ps, 1)

            def v_proj(st, t):
                pair, par, b = st
                if b >= 1 and t == 0:
                    pe.wait_ge(max_done, count(8, pair, par, -1))
                last = product(psW[:, 1, 1, t * P:(t + 1) * P],
                               [(ctxs[:, par, h, k, t * P:(t + 1) * P], wkv_s[:, a, 1, k, :])
                                for k in range(KC) for a, h in HALVES])
                if t == KT - 1:
                    last.then_inc(v_ps, 1)

            def score_rows(st, u):
                pair, par, b = st
                if u == 0:
                    pe.wait_ge(k_rd[par], pair * 16 + 16)
                    pe.wait_ge(q_rd[par], pair * 16 + 16)
                    if b >= 1:
                        pe.wait_ge(mc_done, count(1, pair, par, 0))
                elif u == 1:
                    pe.wait_ge(max_done, count(8, pair, par, 1))
                elif u == 2:
                    pe.wait_ge(vl_done, count(1, pair, par, 1))
                    if b < B - 1:
                        pe.wait_ge(kl_done, count(1, pair, par, 2))
                else:
                    pe.wait_ge(max_done, count(8, pair, par, u - 1))
                for e in range(2):
                    n = 2 * u + e
                    last = nc.tensor.matmul(psW[0:SQ, SLOT[u], e, 0:SK], qst[0:ROW_MAX, par, n, :],
                                            kst[0:ROW_MAX, par, n % G, 0:SK], start=True, stop=True)
                last.then_inc(a_ps, 1)

            def max_turn(st):
                pair, par, b = st
                pe.wait_ge(max_done, count(8, pair, par, 8))
                nc.tensor.transpose(psW[0:NH, 0, 0, 0:SQ], mx[0:SQ, :], ident[0:SQ, 0:SQ]).then_inc(mt_ps, 1)

            def score_cols(st, n):
                pair, par, b = st
                t, g = n // G, n % G
                if n == 0:
                    pe.wait_ge(m_rd[par], pair * 32 + 32)
                if n >= 2 or b >= 1:
                    pe.wait_ge(exp_done, count(12, pair, par, n - 1))
                nc.tensor.matmul(psB[:, n % 2, 0:400], kst[:, par, g, t * P:(t + 1) * P],
                                 qst[:, par, :, :].rearrange("p (a g) q -> p a g q", g=G)[:, :, g, :],
                                 start=True, stop=True).then_inc(b_ps, 1)

            def attend(st, t):
                pair, par, b = st
                if t == 0:
                    pe.wait_ge(vl_done, count(1, pair, par, 1))
                    if b >= 1:
                        pe.wait_ge(o_done, count(1, pair, par, 0))
                if t < 2:
                    pe.wait_ge(pl_p, count(2, pair, par, t + 1))
                else:
                    pe.wait_ge(pl_v, count(1, pair, par, 1))
                ones = key_ones[:, 1 if t == KT - 1 else 0, :]
                for bank, half, probs in ((0, 0, ph), (0, 0, pl), (0, 1, ph), (1, None, ph), (1, None, pl)):
                    for g in range(G):
                        left = ones if half is None else vs[:, par, half, t, g * DH:(g + 1) * DH]
                        last = nc.tensor.matmul(
                            psO[g * DH:(g + 1) * DH, bank, 0:400], left, probs[:, t, g, :],
                            start=(t == 0 and probs is ph and half != 1),
                            stop=(t == KT - 1 and (half == 1 or (half is None and probs is pl))))
                last.then_inc(pv_done, 1)

            def step(m1, s0, p1, p2, p3):
                if p2:
                    k_proj(p2)
                n = u = v = 0
                for what in "1 A 2 B B V B V B V A B B A A B B A B B A B A B A 0 T".split():
                    if what == "B":
                        if s0:
                            score_cols(s0, n)
                        n += 1
                    elif what == "A":
                        if p1:
                            score_rows(p1, u)
                        u += 1
                    elif what == "V":
                        if p1:
                            v_proj(p1, v)
                        v += 1
                    elif what == "T":
                        if p1:
                            max_turn(p1)
                    elif what == "0":
                        if s0:
                            attend(s0, 0)
                    elif m1:
                        attend(m1, int(what))

            pipeline(pe.Fori, step)

            def project(T, c, i, n):
                pe.wait_ge(w_lo, 4)
                if T:
                    pe.wait_ge(x1_done, T)
                if T == 0:
                    pe.wait_ge(ol_done, B)
                if c >= 2:
                    pe.wait_ge(y_done, FIRST[c - 1])
                at = c * CH + i * P
                product(psO[0:n, 0, :], [(oT[:, a, k, at:at + n], wo_s[:, b, k, :])
                                         for k in range(KC) for a, b in HALVES]).then_inc(wo_ps, 1)

            def scales(unit, par):
                pe.wait_ge(wa_done, unit + 1)
                if isinstance(unit, int) and unit == 0:
                    pe.wait_ge(exp_done, 12 * B)
                else:
                    pe.wait_ge(scale_done, unit)
                for e in range(2):
                    last = nc.tensor.matmul(psB[:, e, :], block64[:, :], wa2[:, e * 512:(e + 1) * 512],
                                            start=True, stop=True)
                last.then_inc(quant_ps, 1)

            def square_sums(c):
                pe.wait_ge(acc_done, NM * (c + 1))
                if c == NC - 1:
                    pe.wait_ge(y_done, FIRST[c])
                pe.wait_ge(zl_done, NT + FIRST[min(c + 1, NC - 1)] + len(TILES[min(c + 1, NC - 1)]))
                nc.tensor.matmul(psO[:, 1, 0:CHUNKS[c]], onesf[:, :], acc[:, 0:CHUNKS[c]],
                                 start=True, stop=True).then_inc(rms_ps, 1)

            def down(c):
                pe.wait_ge(w_ready, NU)
                pe.wait_ge(nl_done, NM * (c + 1))
                pe.wait_ge(rt_done, c + 1)
                for T, i, n in tile_list(c):
                    if i < 2:
                        pe.wait_ge(x1_done, FIRST[min(c + 1, NC - 1)] + len(TILES[min(c + 1, NC - 1)]))
                        if T:
                            pe.wait_ge(y_done, T if i == 0 else T - 1)
                    else:
                        pe.wait_ge(y_done, T - 1)
                    product(psO[0:n, i % 2, :],
                            [(hn[:, h, m, i * P:i * P + n], w_ffn[:, NU_GU + m // 2, (m % 2) * D:(m % 2 + 1) * D])
                             for m in range(NM) for h in range(2)]).then_inc(proj_ps, 1)

            scales(0, 0)
            scales(1, 1)
            for c, n in enumerate(CHUNKS):
                tiles = tile_list(c)
                project(*tiles[0][:1], c, *tiles[0][1:])
                for e, (T, i, rows) in enumerate(tiles):
                    if e + 1 < len(tiles):
                        T1, i1, rows1 = tiles[e + 1]
                        project(T1, c, i1, rows1)
                    if T:
                        pe.wait_ge(zl_done, NT + T)
                    if c:
                        pe.wait_ge(y_done, FIRST[c - 1])
                        if c >= 2:
                            pe.wait_ge(rt_done, c - 1)
                    turn(NT + T, 1, rows)
                if c:
                    square_sums(c - 1)
                pe.wait_ge(zl_done, NT + FIRST[c] + len(tiles))

                def body(m0, unit, first):
                    for par in range(2):
                        if unit is not None:
                            scales(unit + par, par)
                        M = m0 + (NM * c + par)
                        if not first:
                            pe.wait_ge(h_done, M - 1)
                        if c == 0:
                            pe.wait_ge(w_ready, m0 + (par + 1))
                        for e in range(2):
                            last = product(psW[:, par, e, 0:n],
                                           [(w_ffn[:, m0 + par, k * 256 + e * P:k * 256 + (e + 1) * P],
                                             zT[:, h, k, 0:n]) for k in range(KC) for h in range(2)])
                        last.then_inc(gu_ps, 1)

                hidden(pe.Fori, c, body)
                if c:
                    down(c - 1)
            square_sums(NC - 1)
            down(NC - 1)


_OUTS = [((B, SQ, D), "float32")]


def constants():
    f16 = np.float16
    slope = np.float32(2.0 ** (-8.0 / NH)) ** np.arange(1, NH + 1, dtype=np.float32)
    order = [g * HPG + a for a in range(HPG) for g in range(G)]
    slope = slope[order].astype(np.float64)
    qaux = np.zeros((P - ROW_AUX, NH, SQ), f16)
    off = -slope[:, None] * np.arange(SQ)[None, :]
    for row, v in ((0, np.repeat(slope[:, None], SQ, 1)), (3, off)):
        hi = v.astype(f16)
        lo = (v - hi.astype(np.float64)).astype(f16)
        if row == 0:
            qaux[0], qaux[1] = hi, lo
        else:
            qaux[3], qaux[4] = hi, lo
    qaux[2] = MASK_Q
    kaux = np.zeros((P - ROW_AUX, G, SKP), f16)
    for row in (3, 4, ROW_MAX - ROW_AUX, ROW_MAX - ROW_AUX + 1):
        kaux[row, :, :SK] = 1.0
    kpos = np.zeros((B, SKP), f16)
    kpos[:, :SK] = np.arange(SK)
    key_ones = np.ones((P, 2, DH), f16)
    key_ones[SK - (KT - 1) * P:, 1] = 0.0
    block = np.kron(np.eye(2), np.full((64, 64), 2.0 ** -7)).astype(f16)
    return {"qaux": qaux, "kaux": kaux, "kpos": kpos, "ident": np.eye(P, dtype=np.float32),
            "block64": block, "key_ones": key_ones}


def layouts(x, ctx_2048, mask_BxS2_bf1, L0_xattn_Wq, L0_xattn_Wk, L0_xattn_Wv, L0_xattn_Wo,
            L0_ffn_w_gate_up, L0_ffn_w_proj):
    def rows(w):
        return w.reshape(KC, P, -1).transpose(1, 0, 2)

    wq = L0_xattn_Wq.reshape(KC, P, G, HPG, DH).transpose(1, 0, 3, 2, 4).reshape(P, KC, D)
    wo = L0_xattn_Wo.reshape(G, HPG, DH, D).transpose(0, 2, 1, 3).reshape(P, HPG, D)
    gu = L0_ffn_w_gate_up.reshape(2, NM, P, KC, P).transpose(1, 4, 3, 0, 2).reshape(NM, P, UNIT)
    p = L0_ffn_w_proj.reshape(D, NM // 2, 2, P).transpose(1, 3, 2, 0).reshape(NM // 2, P, UNIT)
    return {"x": x, "ctxT": ctx_2048.reshape(B, SK, KC, P).transpose(0, 3, 2, 1),
            "mask": mask_BxS2_bf1.view(np.uint8), "wq": wq, "wk": rows(L0_xattn_Wk),
            "wv": rows(L0_xattn_Wv), "wo": wo, "w_gu": gu, "w_p": p}


def kernel(**inputs):
    import concourse.bacc as _bacc
    from concourse.bass_utils import run_bass_kernel_spmd as _run

    nc = _bacc.Bacc("TRN2", target_bir_lowering=False, num_devices=1)
    arrays, args = {}, []
    for name, a in {**layouts(**{k: np.asarray(v) for k, v in inputs.items()}), **constants()}.items():
        a = np.ascontiguousarray(a)
        arrays[f"in_{name}"] = a
        args.append(nc.dram_tensor(f"in_{name}", a.shape, mybir.dt.from_np(a.dtype), kind="ExternalInput").ap())
    for i, (shape, dtype) in enumerate(_OUTS):
        args.append(nc.dram_tensor(f"out_{i}", shape, mybir.dt.from_np(np.dtype(dtype)), kind="ExternalOutput").ap())
    xattn_ffn(nc, *args)
    r = _run(nc, [arrays], core_ids=[0])
    return r.results[0]["out_0"]
```

```python
from contextlib import ExitStack

import concourse.bass as bass
import numpy as np
from concourse import mybir

F32 = mybir.dt.float32
F16 = mybir.dt.float16
BF16 = mybir.dt.bfloat16
U8 = mybir.dt.uint8
ALU = mybir.AluOpType
ACT = mybir.ActivationFunctionType
AX = mybir.AxisListType

P = 128
B, SQ, D = 16, 100, 512
SK = 361
G, HPG, DH = 4, 4, 32
NH = G * HPG
HID = 2048
TOK = B * SQ
KC = D // P
KT = -(-SK // P)
SKP = KT * P
NM = HID // P
CH = 512
CHUNKS = [min(CH, TOK - c * CH) for c in range(-(-TOK // CH))]
TILES = [[min(P, n - i * P) for i in range(-(-n // P))] for n in CHUNKS]
UNIT = 1024
NU_GU, NU = NM, NM + NM * D // UNIT
NC = len(CHUNKS)
W_SPLIT = {(0, 1): 1, (0, 2): 2, (2, 3): 3}
SLOT = (0, 0, 1, 0, 1, 0, 1, 0)
NT = sum(len(t) for t in TILES)
FIRST = [sum(len(t) for t in TILES[:c]) for c in range(NC)]
EARLY = 2
LEAD = EARLY + len(TILES[0])
HALF = NM // 4

WS = 64.0
ZS = 256.0
LN_EPS = 1e-5
RMS_EPS = float(np.finfo(np.float32).eps)
PSHIFT = float(10 * np.log(2))
SCORE_SCALE = 1.0 / float(np.sqrt(DH))
SCALE_MIN = 9.9837779998779297e-09
MASK_Q, MASK_K = 2048.0, 65504.0
ROW_AUX, ROW_MAX = 96, 126


def count(per, pair, parity, extra):
    return pair * (2 * per) + (per * parity + extra)


def xattn_ffn(nc, x, ctxT, mask, wq, wk, wv, wo, w_gu, w_p, qaux, kaux, kpos, ident_h,
              block_h, ones_h, out):
    with ExitStack() as ctx:
        def sb(name, shape, dt):
            return ctx.enter_context(nc.sbuf_tensor(name, shape, dt))

        def sem(name):
            return ctx.enter_context(nc.semaphore(name))

        q_dram = nc.dram_tensor("q_dram", (3 * DH, HPG, G, TOK), F16, kind="Internal").ap()
        k_dram = nc.dram_tensor("k_dram", (B, 3 * DH + 3, G, SKP), F16, kind="Internal").ap()
        any_dram = nc.dram_tensor("any_dram", (B, 1), F32, kind="Internal").ap()

        ident = sb("ident", [P, P], F32)
        block64 = sb("block64", [P, P], F16)
        onesf = sb("onesf", [P, P], F32)
        key_ones = sb("key_ones", [P, 2, DH], F16)
        flag = sb("flag", [P, B], F32)
        minus_half = sb("minus_half", [P, 1], F32)
        oT = sb("oT", [P, 2, HPG, TOK], F16)
        wo_s = sb("wo_s", [P, 2, KC, D], F16)
        xs = sb("xs", [P, 2, 4, D], F32)
        ztile = sb("ztile", [P, KC * CH], F32)
        zrow = sb("zrow", [P, 2, D], F32)
        stats = sb("stats", [P, 2, 6], F32)
        mv = sb("mv", [P, 2, 2], F32)
        ve = sb("ve", [P, 2, 1], F32)
        rstd = sb("rstd", [P, 2, 1], F32)

        def carve(name, words):
            tile, at = sb(name, [P, words], F32), [0]

            def part(n):
                at[0] += n
                assert at[0] <= words
                return tile[:, at[0] - n:at[0]]
            return tile, part, at

        one, part, _ = carve("one", 2 * NM * CH)
        p32 = part(KT * G * 400).rearrange("p (t g c) -> p t g c", t=KT, g=G)
        ph = part(KT * G * 200).bitcast(F16).rearrange("p (t g c) -> p t g c", t=KT, g=G)
        pl = part(KT * G * 200).bitcast(F16).rearrange("p (t g c) -> p t g c", t=KT, g=G)
        ctx32 = part(2 * KC * SKP).rearrange("p (b k s) -> p b k s", b=2, k=KC)
        ctxs = part(2 * KC * SKP).bitcast(F16).rearrange("p (b h k s) -> p b h k s", b=2, h=2, k=KC)
        h32 = one[:, 0:NM * CH].rearrange("p (m n) -> p m n", m=NM)
        hn = one[:, NM * CH:2 * NM * CH].bitcast(F16).rearrange("p (h m n) -> p h m n", h=2, m=NM)
        w32 = [one[:, 0:2048].rearrange("p (k n) -> p k n", k=KC),
               one[:, 2048:2560].rearrange("p (k n) -> p k n", k=KC),
               one[:, 2560:3072].rearrange("p (k n) -> p k n", k=KC),
               one[:, 3072:5120].rearrange("p (k n) -> p k n", k=KC)]
        maskf = one[0:B, 5120:5120 + SK]
        maskb = one[0:B, 5504:5504 + SK]
        kvar = one[0:B, 5888:5888 + 3 * SKP // 2].bitcast(F16).rearrange("p (r s) -> p r s", r=3)
        kposs = one[0:B, 6528:6528 + SKP // 2].bitcast(F16)
        mask8 = one[0:B, 6784:6784 + 96].bitcast(U8)[:, 0:SK]

        two, part, _ = carve("two", NU * UNIT // 2)
        w_ffn = two[:, :].bitcast(BF16).rearrange("p (u n) -> p u n", u=NU)
        wq_s = part(KC * D).bitcast(F16).rearrange("p (h k n) -> p h k n", h=2, k=KC)
        wkv_s = part(KC * 2 * P).bitcast(F16).rearrange("p (h v k n) -> p h v k n", h=2, v=2, k=KC)
        kst = part(G * SKP).bitcast(F16).rearrange("p (b g s) -> p b g s", b=2, g=G)
        qst = part(NH * SQ).bitcast(F16).rearrange("p (b n q) -> p b n q", b=2, n=NH)
        vs = part(2 * KT * P).bitcast(F16).rearrange("p (b h t n) -> p b h t n", b=2, h=2, t=KT)
        qstage = part(2 * HPG * CH).bitcast(F16).rearrange("p (b h a n) -> p b h a n", b=2, h=2, a=HPG)
        kh_s = part(SKP).bitcast(F16).rearrange("p (h s) -> p h s", h=2)
        rsum = part(400)
        o32 = part(400)

        wraw = sb("wraw", [P, 2, UNIT], F32)
        wtmp = sb("wtmp", [P, 4, UNIT], BF16)
        ztmp = ztile[:, :].bitcast(BF16).rearrange("p (i n) -> p i n", i=4)
        zT = [ztile[:, :].bitcast(F16).rearrange("p (h k n) -> p h k n", h=2, k=KC),
              wtmp[:, :, :].rearrange("p i n -> p (i n)").bitcast(F16
              ).rearrange("p (h k n) -> p h k n", h=2, k=KC)]
        wb, wa2, wsg, wsc = ([wtmp[:, i, :], ztmp[:, i, :]] for i in range(4))
        hn_last = wraw[:, :, :].rearrange("p a n -> p (a n)")[:, 0:NM * CHUNKS[-1]].bitcast(F16
                  ).rearrange("p (h m n) -> p h m n", h=2, m=NM)
        mx = sb("mx", [P, NH], F32)
        mc = sb("mc", [NH, SQ], F32)
        mrow = sb("mrow", [NH, 2, SQ], F16)
        anyk = sb("anyk", [B, 2], F32)
        sil = sb("sil", [P, 2, CH], F32)
        sqb = sb("sqb", [P, 2, CH], F32)
        acc = sb("acc", [P, CH], F32)
        msq = sb("msq", [P, CH // P], F32)
        rinv = sb("rinv", [P, CH // P], F32)
        rdiag = sb("rdiag", [P, CH], F32)

        psW = ctx.enter_context(nc.psum_tensor("psW", [P, 2, 2, 512], F32))
        psB = ctx.enter_context(nc.psum_tensor("psB", [P, 2, 512], F32))
        psO = ctx.enter_context(nc.psum_tensor("psO", [P, 2, 512], F32))

        ident_ld, const_ld, flag_w, flag_ld, any_done, kvar_done = (
            sem(n) for n in "ident_ld const_ld flag_w flag_ld any_done kvar_done".split())
        mask_ld, mask_f, mask_b, w_hi, w_lo, set_done = (
            sem(n) for n in "mask_ld mask_f mask_b w_hi w_lo set_done".split())
        stats_done, aggr_done, eps_added, rstd_done, z_done, zt_ps, zh_done, zl_done = (
            sem(n) for n in "stats_done aggr_done eps_added rstd_done z_done zt_ps zh_done zl_done".split())
        q_ps, qh_done, ql_done, wo_ps, x1_done = (
            sem(n) for n in "q_ps qh_done ql_done wo_ps x1_done".split())
        ctxh_done, ctxl_done, k_ps, kh_done, kl_done, v_ps, vh_done, vl_done, k_wr = (
            sem(n) for n in "ctxh_done ctxl_done k_ps kh_done kl_done v_ps vh_done vl_done k_wr".split())
        a_ps, max_done, mt_ps, mc_done, mh_done, ml_done, b_ps, exp_done = (
            sem(n) for n in "a_ps max_done mt_ps mc_done mh_done ml_done b_ps exp_done".split())
        ph_v, ph_a, pl_p, pl_v, pv_done, rs_done, o_done, oh_done, ol_done = (
            sem(n) for n in "ph_v ph_a pl_p pl_v pv_done rs_done o_done oh_done ol_done".split())
        wb_done, wa_done, wg_done, quant_ps, scale_done, mk_done, sw_done, wh_done, wd_done, w_ready = (
            sem(n) for n in ("wb_done wa_done wg_done quant_ps scale_done mk_done sw_done wh_done "
                             "wd_done w_ready").split())
        gu_ps, sil_done, h_done, sq_done, acc_zero, acc_done, rms_ps, rt_done, rinv_done, rd_done, rb_ps = (
            sem(n) for n in ("gu_ps sil_done h_done sq_done acc_zero acc_done rms_ps rt_done "
                             "rinv_done rd_done rb_ps").split())
        n_done, nh_done, nl_done, proj_ps, y_done = (
            sem(n) for n in "n_done nh_done nl_done proj_ps y_done".split())
        x_ld = [sem(f"x_ld{i}") for i in range(8)]
        y_st = [sem(f"y_st{i}") for i in range(8)]
        ctx_ld = [sem(f"ctx_ld{i}") for i in range(2)]
        k_rd = [sem(f"k_rd{i}") for i in range(2)]
        q_rd = [sem(f"q_rd{i}") for i in range(2)]
        m_rd = [sem(f"m_rd{i}") for i in range(2)]
        w_ld = [sem(f"w_ld{i}") for i in range(4)]
        q_wr = [sem(f"q_wr{i}") for i in range(2)]
        raw_ld = [sem(f"raw_ld{i}") for i in range(2)]

        x_rows = x.rearrange("b q d -> (b q) d")
        out_rows = out.rearrange("b q d -> (b q) d")

        def tile_list(c):
            return [(FIRST[c] + i, i, n) for i, n in enumerate(TILES[c])]

        def x_loads(rnd, c, i):
            before = sum(1 for r in range(2) for cc in range(NC) if (r, cc) < (rnd, c)
                         and cc % 2 == c % 2 and i < len(TILES[cc]))
            return 16 * (before + 1)

        def pipeline(fori, step, quantise=None):
            for j in (-3, -2, -1, 0, 1):
                step(*(known(j + d) for d in range(-1, 4)))
                if j == -3 and quantise:
                    for unit in range(EARLY):
                        quantise(unit)
            with fori(1, B // 2 - 2) as pair:
                for parity in range(2):
                    step(*((pair + (parity + d) // 2, (parity + d) % 2, 2) for d in range(-1, 4)))
            for j in range(B - 4, B + 1):
                step(*(known(j + d) for d in range(-1, 4)))

        def known(b):
            return (b // 2, b % 2, b) if 0 <= b < B else None

        def q_written(c):
            return 48 * (c // 2 + 1)

        def starts(c, m, n):
            return c == 0 and isinstance(m, int) and m < n

        def chunk_end(c):
            return FIRST[c] + len(TILES[c])

        def sums_at(c):
            return psO[:, 1, 0:4] if c < NC - 1 else psW[:, 0, 0, 0:4]

        def spread_to(c):
            return psO[:, 1, 0:CHUNKS[c]] if c < NC - 1 else psW[:, 0, 0, 0:CHUNKS[c]]

        def halves(c):
            return hn if c < NC - 1 else hn_last

        def share(c):
            return 4 if c < NC - 1 else 2

        def feed_forward(fori, turn_in, pairs, normed, down, beside):
            turn_in(0, EARLY)
            pairs(0, 0, LEAD)
            with fori(1, NM // 2) as i:
                pairs(i, 0, 2 * i + LEAD)
            turn_in(1, LEAD + NM)
            for c in range(1, NC):
                normed(0, c, True)
                with fori(1, NM // share(c)) as i:
                    normed(i, c, False)
                if c < NC - 1:
                    down(c - 1)
                    for e in range(HALF):
                        nxt = tile_list(c + 1)
                        beside(HALF + e, c, nxt[e] if e < len(nxt) else None)

        block = ctx.enter_context(nc.Block())

        @block.sync
        def _(sp):
            def wait(*waits):
                waits = [(s, v if isinstance(v, int) else sp.snap(sp.to_reg(v))) for s, v in waits]
                for s, v in waits:
                    sp.wait_ge(s, v)

            def load_x(rnd, c, only=None):
                for T, i, n in tile_list(c):
                    if only not in (None, i):
                        continue
                    sl = (c % 2) * 4 + i
                    if rnd == 0 and c >= 2:
                        sp.wait_ge(z_done, FIRST[c - 2] + i + 1)
                    if rnd == 1 and c < 2:
                        sp.wait_ge(z_done, NT)
                    if rnd == 1 and c >= 2:
                        sp.wait_ge(y_st[sl], 16)
                    sp.dma_start(xs[0:n, c % 2, i, :], x_rows[T * P:T * P + n, :]).then_inc(x_ld[sl], 16)

            load_x(0, 0)
            sp.dma_start(ident[:, :], ident_h).then_inc(ident_ld, 16)
            sp.dma_start(w32[0], wq).then_inc(w_ld[0], 16)
            sp.dma_start(mask8, mask).then_inc(mask_ld, 16)
            sp.dma_start(kposs, kpos).then_inc(mask_ld, 16)
            for i, w in ((1, wk), (2, wv)):
                sp.dma_start(w32[i], w).then_inc(w_ld[i], 16)
            load_x(0, 1)
            sp.dma_start(w32[3], wo).then_inc(w_ld[3], 16)
            for b in range(2):
                sp.dma_start(kst[ROW_AUX:P, b, :, :], kaux).then_inc(const_ld, 16)
                sp.dma_start(qst[ROW_AUX:P, b, :, :], qaux).then_inc(const_ld, 16)
            sp.dma_start(block64[:, :], block_h).then_inc(const_ld, 16)
            sp.dma_start(key_ones[:, :, :], ones_h).then_inc(const_ld, 16)
            sp.wait_ge(any_done, 2)
            sp.dma_start(any_dram, anyk[:, 1:2]).then_inc(flag_w, 16)
            sp.wait_ge(kvar_done, 4)
            for g in range(G):
                sp.dma_start(k_dram[:, 3 * DH:, g, :], kvar).then_inc(flag_w, 16)
            sp.wait_ge(flag_w, 16 * (G + 1))
            sp.dma_start(flag[:, :], any_dram.rearrange("b a -> a b").to_broadcast([P, B])
                         ).then_inc(flag_ld, 16)
            sp.wait_ge(set_done, 4)

            def load_ctx(st):
                pair, par, b = st
                if b >= 2:
                    wait((ctxh_done, count(1, pair, par, -1)),
                         (ctxl_done, count(1, pair, par, -1)))
                sp.dma_start(ctx32[:, par, :, 0:SK], ctxT[2 * pair + par]).then_inc(ctx_ld[par], 16)

            load_ctx(known(0))
            load_ctx(known(1))

            def fetch(unit, par, src, base, first):
                if not first:
                    wait((wb_done, unit - 1), (wa_done, unit - 1), (wg_done, unit - 1))
                sp.dma_start(wraw[:, par, :], src[unit - base]).then_inc(raw_ld[par], 16)

            for c, n in enumerate(CHUNKS):
                if c + 2 < NC:
                    load_x(0, c + 2)
                if c < EARLY:
                    fetch(c, c, w_gu, 0, True)
                for r, half in ((0, 0), (2, 0), (1, 1)):
                    sp.wait_ge((qh_done, ql_done)[half], HPG * (c + 1))
                    sp.dma_start(q_dram[r * DH:(r + 1) * DH, :, :, c * CH:c * CH + n]
                                 .rearrange("d a g t -> g d a t"),
                                 qstage[:, c % 2, half, :, 0:n]).then_inc(q_wr[c % 2], 16)
            for c in (NC - 2, NC - 1):
                sp.wait_ge(q_wr[c % 2], q_written(c))

            def write_k(st):
                pair, par, b = st
                for r, half in ((0, 0), (1, 0), (2, 1)):
                    wait(((kh_done, kl_done)[half], count(1, pair, par, 1)))
                    sp.dma_start(k_dram[2 * pair + par, r * DH:(r + 1) * DH].rearrange("d g s -> g d s"),
                                 kh_s[:, half, :]).then_inc(k_wr, 16)

            def fill_stacks(st):
                pair, par, b = st
                wait((k_wr, count(48, pair, par, 48)),
                     *([(b_ps, count(12, pair, par, -12))] if b >= 2 else []))
                sp.dma_start(kst[0:3 * DH + 3, par, :, :], k_dram[2 * pair + par]).then_inc(k_rd[par], 16)
                sp.dma_start(qst[0:3 * DH, par, :, :], q_dram[:, :, :, bass.ds((2 * pair + par) * SQ, SQ)]
                             .rearrange("p a g t -> p (a g) t")).then_inc(q_rd[par], 16)

            def step(m1, s0, p1, p2, p3):
                if p3 and p3[2] >= 2:
                    load_ctx(p3)
                if p2:
                    write_k(p2)
                    fill_stacks(p2)

            pipeline(sp.Fori, step)

            load_x(1, 0)
            load_x(1, 1)
            with sp.Fori(1, NU_GU // 2) as i:
                for par in range(2):
                    fetch(i * 2 + par, par, w_gu, 0, False)
            with sp.Fori(NU_GU // 2, NU // 2) as i:
                for par in range(2):
                    fetch(i * 2 + par, par, w_p, NU_GU, False)
            for c in range(NC):
                for T, i, n in tile_list(c):
                    sp.wait_ge(y_done, T + 1)
                    sp.dma_start(out_rows[T * P:T * P + n, :], xs[0:n, c % 2, i, :]
                                 ).then_inc(y_st[(c % 2) * 4 + i], 16)
                    if c + 2 < NC and i:
                        load_x(1, c + 2, i - 1)
                if c + 2 < NC:
                    load_x(1, c + 2, i)
            for sl in range(8):
                sp.wait_ge(y_st[sl], 16 * sum(1 for c in range(NC) if c % 2 == sl // 4
                                              and sl % 4 < len(TILES[c])))

        @block.gpsimd
        def _(pool):
            nc.gpsimd.memset(minus_half[:, :], -0.5).then_inc(set_done, 1)
            nc.gpsimd.memset(onesf[:, :], 1.0).then_inc(set_done, 1)
            for b in range(2):
                nc.gpsimd.memset(ctx32[:, b, :, SK:SKP], 0.0).then_inc(set_done, 1)
            pool.wait_ge(set_done, 4)

            def rstd_of(k, n):
                pool.wait_ge(aggr_done, k + 1)
                if k >= 2:
                    pool.wait_ge(z_done, k - 1)
                nc.gpsimd.tensor_scalar(ve[0:n, k % 2, :], mv[0:n, k % 2, 1:2], 1.0, LN_EPS,
                                        ALU.mult, ALU.add).then_inc(eps_added, 1)
                pool.wait_ge(eps_added, k + 1)
                nc.gpsimd.tensor_tensor(rstd[0:n, k % 2, :], ve[0:n, k % 2, :], minus_half[0:n, :],
                                        ALU.pow).then_inc(rstd_done, 1)


            def ctx_low(st):
                pair, par, b = st
                pool.wait_ge(ctxh_done, count(1, pair, par, 1))
                if b >= 2:
                    pool.wait_ge(v_ps, count(1, pair, par, -1))
                nc.gpsimd.tensor_tensor(ctxs[:, par, 1, :, :], ctx32[:, par, :, :], ctxs[:, par, 0, :, :],
                                        ALU.subtract).then_inc(ctxl_done, 1)

            for c in range(NC):
                for T, i, n in tile_list(c):
                    rstd_of(T, n)
            ctx_low(known(0))
            ctx_low(known(1))

            def p_low(st, t):
                pair, par, b = st
                if t == 0:
                    pool.wait_ge(ph_v, count(1, pair, par, 1))
                else:
                    pool.wait_ge(ph_a, count(2, pair, par, 1))
                if b >= 1:
                    pool.wait_ge(pv_done, count(3, pair, par, t - 2))
                nc.gpsimd.tensor_tensor(pl[:, t, :, :], p32[:, t, :, :], ph[:, t, :, :],
                                        ALU.subtract).then_inc(pl_p, 1)

            def step(m1, s0, p1, p2, p3):
                if s0:
                    p_low(s0, 0)
                if p3 and p3[2] >= 2:
                    ctx_low(p3)
                if s0:
                    p_low(s0, 1)

            def add_weights(unit, par):
                pool.wait_ge(wd_done, unit + 1)
                nc.gpsimd.tensor_tensor(w_ffn[:, unit, :], wb[par], wsg[par], ALU.add).then_inc(w_ready, 1)

            pipeline(pool.Fori, step, lambda unit: add_weights(unit, unit))

            def add_squares(c, m, par):
                n = CHUNKS[c]
                pool.wait_ge(sq_done, m + (NM * c + 1))
                if not starts(c, m, 1):
                    pool.wait_ge(acc_done, m + NM * c)
                nc.gpsimd.tensor_tensor(acc[:, 0:n], acc[:, 0:n], sqb[:, par, 0:n], ALU.add
                                        ).then_inc(acc_done, 1)

            def inverse_root(c):
                pool.wait_ge(rt_done, c + 1)
                if c:
                    pool.wait_ge(rd_done, c)
                rows, cols = min(P, CHUNKS[c]), len(TILES[c])
                nc.gpsimd.tensor_tensor(rinv[0:rows, 0:cols], msq[0:rows, 0:cols],
                                        minus_half[0:rows, :].to_broadcast([rows, cols]),
                                        ALU.pow).then_inc(rinv_done, 1)

            def zero(c):
                if c:
                    pool.wait_ge(rms_ps, c)
                nc.gpsimd.memset(acc[:, :], 0.0).then_inc(acc_zero, 1)
                if c:
                    inverse_root(c - 1)
                pool.wait_ge(acc_zero, c + 1)

            def turn_in(c, unit):
                for T, i, rows in tile_list(c):
                    rstd_of(NT + T, rows)
                    if unit + i < NU:
                        add_weights(unit + i, i % 2)
                if c == 0:
                    zero(0)

            def pairs(i, c, unit):
                for par in range(2):
                    add_squares(c, 2 * i + par, par)
                    add_weights(unit + par, par)

            def normed(i, c, begin):
                if begin:
                    zero(c)
                for par in range(2):
                    add_squares(c, 2 * i + par, par)

            def beside(i, c, tile):
                if tile:
                    rstd_of(NT + tile[0], tile[2])
                for par in range(2):
                    add_squares(c, 2 * i + par, par)

            feed_forward(pool.Fori, turn_in, pairs, normed, lambda c: None, beside)
            inverse_root(NC - 1)

        @block.scalar
        def _(act):
            def fixed(v):
                return v if isinstance(v, int) else act.snap(act.to_reg(v))

            def z_high(k, bank, at, n, scale, dst):
                act.wait_ge(zt_ps, k + 1)
                nc.scalar.activation(dst[:, 0, :, at:at + n],
                                     psO[:, bank, :].rearrange("p (k t) -> p k t", k=KC)[:, :, 0:n],
                                     ACT.Copy, scale=scale).then_inc(zh_done, 1)

            w_high = (wq_s[:, 0, :, :], wkv_s[:, 0, 0, :, :], wkv_s[:, 0, 1, :, :], wo_s[:, 0, :, :])

            def split_w(i):
                act.wait_ge(w_ld[i], 16)
                nc.scalar.activation(w_high[i], w32[i], ACT.Copy, scale=WS).then_inc(w_hi, 1)

            def z_in(c, i):
                if c < NC and i < len(TILES[c]):
                    if c >= 2 and i == 0:
                        act.wait_ge(q_ps, HPG * (c - 1))
                    T = FIRST[c] + i
                    z_high(T, T % 2, i * P, TILES[c][i], 1.0, zT[c % 2])

            def ctx_high(st):
                pair, par, b = st
                act.wait_ge(ctx_ld[par], pair * 16 + 16)
                if b >= 2:
                    act.wait_ge(v_ps, count(1, pair, par, -1))
                    act.wait_ge(ctxl_done, count(1, pair, par, -1))
                nc.scalar.activation(ctxs[:, par, 0, :, :], ctx32[:, par, :, :], ACT.Copy).then_inc(ctxh_done, 1)

            for i in range(len(TILES[0])):
                z_in(0, i)
                if i == 2:
                    split_w(0)
            for c, cols in enumerate(CHUNKS):
                if c >= 2:
                    act.wait_ge(q_wr[c % 2], q_written(c - 2))
                for hh in range(HPG):
                    act.wait_ge(q_ps, HPG * c + hh + 1)
                    nc.scalar.activation(qstage[:, c % 2, 0, hh, 0:cols], psW[:, hh // 2, hh % 2, 0:cols],
                                         ACT.Copy, scale=SCORE_SCALE / WS).then_inc(qh_done, 1)
                    z_in(c + 1, hh)
                    if (c, hh) in W_SPLIT:
                        split_w(W_SPLIT[c, hh])
                    if c == NC - 2 and hh < 2:
                        ctx_high(known(hh))

            def k_high(st):
                pair, par, b = st
                act.wait_ge(k_ps, count(1, pair, par, 1))
                if b >= 1:
                    act.wait_ge(k_wr, count(48, pair, par, 0))
                else:
                    act.wait_ge(flag_ld, 16)
                nc.scalar.activation(kh_s[:, 0, :], psW[:, 1, 0, 0:SKP], ACT.Copy,
                                     scale=flag[:, bass.ds(fixed(2 * pair + par), 1)]).then_inc(kh_done, 1)

            def v_high(st):
                pair, par, b = st
                act.wait_ge(v_ps, count(1, pair, par, 1))
                if b >= 2:
                    act.wait_ge(pv_done, count(3, pair, par, -3))
                nc.scalar.activation(vs[:, par, 0, :, :],
                                     psW[:, 1, 1, 0:SKP].rearrange("p (t n) -> p t n", t=KT),
                                     ACT.Copy, scale=1.0 / WS).then_inc(vh_done, 1)

            def exp(st, t, g):
                pair, par, b = st
                n = 4 * t + g
                act.wait_ge(b_ps, count(12, pair, par, n + 1))
                if b == 0 and n == 0:
                    act.wait_ge(w_hi, 4)
                    act.wait_ge(w_lo, 4)
                    act.wait_ge(flag_w, 16 * (G + 1))
                if b >= 1 and g == 0:
                    if t < 2:
                        act.wait_ge(pl_p, count(2, pair, par, t - 1))
                    else:
                        act.wait_ge(pl_v, count(1, pair, par, 0))
                nc.scalar.activation(p32[:, t, g, :], psB[:, n % 2, 0:400], ACT.Exp).then_inc(exp_done, 1)

            def p_high(st, t):
                pair, par, b = st
                act.wait_ge(exp_done, count(12, pair, par, 4 * t + 4))
                if b >= 1:
                    act.wait_ge(pv_done, count(3, pair, par, t - 2))
                nc.scalar.activation(ph[:, t, :, :], p32[:, t, :, :], ACT.Copy).then_inc(ph_a, 1)

            def max_rows(st):
                pair, par, b = st
                for half in range(2):
                    act.wait_ge((mh_done, ml_done)[half], count(1, pair, par, 1))
                    act.dma_start(qst[ROW_MAX + half:ROW_MAX + half + 1, par, :, :],
                                  mrow[:, half, :]).then_inc(m_rd[par], 16)

            def o_high(st):
                pair, par, b = st
                act.wait_ge(o_done, count(1, pair, par, 1))
                nc.scalar.activation(oT[:, 0, :, bass.ds(fixed((2 * pair + par) * SQ), SQ)],
                                     o32.rearrange("p (a q) -> p a q", a=HPG), ACT.Copy).then_inc(oh_done, 1)

            def step(m1, s0, p1, p2, p3):
                if p2:
                    k_high(p2)
                if s0:
                    for g in range(G):
                        exp(s0, 0, g)
                if p1:
                    v_high(p1)
                if m1:
                    o_high(m1)
                if s0:
                    exp(s0, 1, 0)
                    exp(s0, 1, 1)
                if p3 and p3[2] >= 2:
                    ctx_high(p3)
                if s0:
                    exp(s0, 1, 2)
                    exp(s0, 1, 3)
                    p_high(s0, 1)
                    for g in range(G):
                        exp(s0, 2, g)
                    p_high(s0, 2)
                if p1:
                    max_rows(p1)

            def late(unit):
                return not isinstance(unit, int) or unit >= 2

            def quant_abs(unit, par):
                act.wait_ge(raw_ld[par], (unit - par) * 8 + 16)
                if late(unit):
                    act.wait_ge(wh_done, unit - 1)
                nc.scalar.activation(wa2[par], wraw[:, par, :], ACT.Abs, scale=2.0).then_inc(wa_done, 1)

            def quant_sign(unit, par):
                if late(unit):
                    act.wait_ge(w_ready, unit - 1)
                nc.scalar.activation(wb[par], wraw[:, par, :], ACT.Copy).then_inc(wb_done, 1)
                nc.scalar.activation(wsg[par], wraw[:, par, :], ACT.Sign).then_inc(wg_done, 1)

            def quant(unit, par):
                quant_abs(unit, par)
                quant_sign(unit, par)

            pipeline(act.Fori, step, lambda unit: quant(unit, unit))

            def norm_high(c, m):
                act.wait_ge(n_done, m + (NM * c + 1))
                m = fixed(m)
                nc.scalar.activation(halves(c)[:, 0, m, 0:CHUNKS[c]], h32[:, m, 0:CHUNKS[c]], ACT.Copy
                                     ).then_inc(nh_done, 1)

            def silu(c, m, par):
                n = CHUNKS[c]
                act.wait_ge(gu_ps, m + (NM * c + 1))
                if not starts(c, m, 2):
                    act.wait_ge(h_done, m + (NM * c - 1))
                nc.scalar.activation(sil[:, par, 0:n], psW[:, par, 0, 0:n], ACT.Silu,
                                     scale=1.0 / ZS).then_inc(sil_done, 1)

            def square(c, m, par):
                n = CHUNKS[c]
                act.wait_ge(h_done, m + (NM * c + 1))
                if not starts(c, m, 2):
                    act.wait_ge(acc_done, m + (NM * c - 1))
                nc.scalar.activation(sqb[:, par, 0:n], h32[:, fixed(m), 0:n], ACT.Square
                                     ).then_inc(sq_done, 1)

            def turn_in(c, unit):
                for T, i, rows in tile_list(c):
                    if unit + i + 1 < NU:
                        quant(unit + i + 1, (i + 1) % 2)
                    z_high(NT + T, 1, T * P, rows, ZS, oT)

            def pairs(i, c, unit):
                for par in range(2):
                    silu(c, 2 * i + par, par)
                    quant_abs(unit + par + 1, 1 - par)
                    square(c, 2 * i + par, par)
                    quant_sign(unit + par + 1, 1 - par)

            def normed(i, c, begin):
                if begin and c >= 2:
                    act.wait_ge(proj_ps, FIRST[c - 1])
                for j in range(share(c)):
                    norm_high(c - 1, share(c) * i + j)
                for par in range(2):
                    silu(c, 2 * i + par, par)
                for par in range(2):
                    square(c, 2 * i + par, par)

            def beside(i, c, tile):
                silu(c, 2 * i, 0)
                square(c, 2 * i, 0)
                if tile:
                    z_high(NT + tile[0], 1, tile[0] * P, tile[2], ZS, oT)
                silu(c, 2 * i + 1, 1)
                square(c, 2 * i + 1, 1)

            quant(EARLY, EARLY % 2)
            feed_forward(act.Fori, turn_in, pairs, normed, lambda c: None, beside)
            act.wait_ge(w_ready, NU)
            with act.Fori(0, NM) as m:
                norm_high(NC - 1, m)

        @block.vector
        def _(dve):
            V = nc.vector

            def normalise(k, c, i, n, second):
                if second:
                    dve.wait_ge(x1_done, k - NT + 1)
                else:
                    dve.wait_ge(x_ld[(c % 2) * 4 + i], x_loads(0, c, i))
                if k >= 2:
                    dve.wait_ge(rstd_done, k - 1)
                    dve.wait_ge(z_done, k - 1)
                V.bn_stats(stats[0:n, k % 2, :], xs[0:n, c % 2, i, :]).then_inc(stats_done, 1)
                dve.wait_ge(stats_done, k + 1)
                V.bn_aggr(mv[0:n, k % 2, :], stats[0:n, k % 2, :]).then_inc(aggr_done, 1)

            def z_of(k, c, i, n):
                dve.wait_ge(rstd_done, k + 1)
                if k >= 2:
                    dve.wait_ge(zt_ps, k - 1)
                V.tensor_scalar(zrow[0:n, k % 2, :], xs[0:n, c % 2, i, :], mv[0:n, k % 2, 0:1],
                                rstd[0:n, k % 2, :], ALU.subtract, ALU.mult).then_inc(z_done, 1)

            def z_low(k, bank, at, n, scale, dst):
                dve.wait_ge(zh_done, k + 1)
                V.scalar_tensor_tensor(out=dst[:, 1, :, at:at + n],
                                       in0=psO[:, bank, :].rearrange("p (k t) -> p k t", k=KC)[:, :, 0:n],
                                       scalar=scale, in1=dst[:, 0, :, at:at + n],
                                       op0=ALU.mult, op1=ALU.subtract).then_inc(zl_done, 1)

            w_low = (wq_s[:, :, :, :], wkv_s[:, :, 0, :, :], wkv_s[:, :, 1, :, :], wo_s[:, :, :, :])

            def split_w(i):
                dve.wait_ge(w_hi, i + 1)
                V.scalar_tensor_tensor(out=w_low[i][:, 1, :, :], in0=w32[i], scalar=WS,
                                       in1=w_low[i][:, 0, :, :], op0=ALU.mult, op1=ALU.subtract
                                       ).then_inc(w_lo, 1)

            def masks():
                V.memset(kvar, 0.0).then_inc(kvar_done, 1)
                dve.wait_ge(mask_ld, 32)
                V.tensor_copy(maskf, mask8).then_inc(mask_f, 1)
                dve.wait_ge(mask_f, 1)
                V.tensor_reduce(anyk[:, 0:1], maskf, AX.X, ALU.max).then_inc(any_done, 1)
                V.tensor_scalar(maskb, maskf, 1.0, MASK_K, ALU.subtract, ALU.mult).then_inc(mask_b, 1)
                dve.wait_ge(any_done, 1)
                V.tensor_scalar(anyk[:, 1:2], anyk[:, 0:1], 1.0 / WS, None, ALU.mult).then_inc(any_done, 1)
                dve.wait_ge(kvar_done, 1)
                for r in range(2):
                    V.tensor_scalar(kvar[:, r, :], kposs, anyk[:, 0:1], None, ALU.mult).then_inc(kvar_done, 1)
                dve.wait_ge(mask_b, 1)
                V.tensor_scalar(kvar[:, 2, 0:SK], maskb, anyk[:, 0:1], None, ALU.mult).then_inc(kvar_done, 1)

            def z_in(c, i):
                if c < NC and i < len(TILES[c]):
                    T = FIRST[c] + i
                    normalise(T, c, i, TILES[c][i], False)
                    z_of(T, c, i, TILES[c][i])
                if c < NC and 0 < i <= len(TILES[c]):
                    T = FIRST[c] + i - 1
                    z_low(T, T % 2, (i - 1) * P, TILES[c][i - 1], 1.0, zT[c % 2])

            for i in range(len(TILES[0]) + 1):
                z_in(0, i)
                if i == len(TILES[0]) - 1:
                    split_w(0)
            for c, cols in enumerate(CHUNKS):
                for hh in range(HPG):
                    z_in(c + 1, hh)
                    dve.wait_ge(qh_done, HPG * c + hh + 1)
                    if c >= 2 and hh == 0:
                        dve.wait_ge(q_wr[c % 2], q_written(c - 2))
                    V.scalar_tensor_tensor(out=qstage[:, c % 2, 1, hh, 0:cols],
                                           in0=psW[:, hh // 2, hh % 2, 0:cols], scalar=SCORE_SCALE / WS,
                                           in1=qstage[:, c % 2, 0, hh, 0:cols],
                                           op0=ALU.mult, op1=ALU.subtract).then_inc(ql_done, 1)
                    if c == 0 and hh == 0:
                        masks()
                    if (c, hh) in W_SPLIT:
                        split_w(W_SPLIT[c, hh])
                z_in(c + 1, HPG)

            def k_low(st):
                pair, par, b = st
                dve.wait_ge(kh_done, count(1, pair, par, 1))
                if b >= 1:
                    dve.wait_ge(k_wr, count(48, pair, par, 0))
                V.scalar_tensor_tensor(out=kh_s[:, 1, :], in0=psW[:, 1, 0, 0:SKP],
                                       scalar=flag[:, bass.ds(2 * pair + par, 1)], in1=kh_s[:, 0, :],
                                       op0=ALU.mult, op1=ALU.subtract).then_inc(kl_done, 1)

            def v_low(st):
                pair, par, b = st
                dve.wait_ge(vh_done, count(1, pair, par, 1))
                V.scalar_tensor_tensor(out=vs[:, par, 1, :, :],
                                       in0=psW[:, 1, 1, 0:SKP].rearrange("p (t n) -> p t n", t=KT),
                                       scalar=1.0 / WS, in1=vs[:, par, 0, :, :],
                                       op0=ALU.mult, op1=ALU.subtract).then_inc(vl_done, 1)

            def maxima(st, u):
                pair, par, b = st
                dve.wait_ge(a_ps, count(8, pair, par, u + 1))
                if b >= 1 and u == 0:
                    dve.wait_ge(mt_ps, count(1, pair, par, 0))
                V.tensor_reduce(mx[0:SQ, 2 * u:2 * u + 2], psW[0:SQ, SLOT[u], :, 0:SK], AX.X, ALU.max,
                                negate=True).then_inc(max_done, 1)

            def max_split(st):
                pair, par, b = st
                dve.wait_ge(mt_ps, count(1, pair, par, 1))
                if b >= 1:
                    before = pair if par else pair - 1
                    dve.wait_ge(ml_done, count(1, pair, par, 0))
                    dve.wait_ge(m_rd[1 - par], before * 32 + 32)
                V.tensor_scalar(mc[:, :], psW[0:NH, 0, 0, 0:SQ], PSHIFT, None, ALU.add).then_inc(mc_done, 1)
                dve.wait_ge(mc_done, count(1, pair, par, 1))
                V.tensor_copy(mrow[:, 0, :], mc[:, :]).then_inc(mh_done, 1)
                dve.wait_ge(mh_done, count(1, pair, par, 1))
                V.tensor_tensor(mrow[:, 1, :], mc[:, :], mrow[:, 0, :], ALU.subtract).then_inc(ml_done, 1)

            def p_high(st, t):
                pair, par, b = st
                dve.wait_ge(exp_done, count(12, pair, par, 4 * t + 4))
                if b >= 1:
                    dve.wait_ge(pv_done, count(3, pair, par, t - 2))
                V.tensor_copy(ph[:, t, :, :], p32[:, t, :, :]).then_inc(ph_v, 1)

            def p_low(st, t):
                pair, par, b = st
                dve.wait_ge(ph_a, count(2, pair, par, 2))
                if b >= 1:
                    dve.wait_ge(pv_done, count(3, pair, par, t - 2))
                V.tensor_tensor(pl[:, t, :, :], p32[:, t, :, :], ph[:, t, :, :], ALU.subtract).then_inc(pl_v, 1)

            def attended(st):
                pair, par, b = st
                dve.wait_ge(pv_done, count(3, pair, par, 3))
                if b >= 1:
                    dve.wait_ge(o_done, count(1, pair, par, 0))
                V.reciprocal(rsum, psO[:, 1, 0:400]).then_inc(rs_done, 1)
                dve.wait_ge(rs_done, count(1, pair, par, 1))
                if b >= 1:
                    dve.wait_ge(oh_done, count(1, pair, par, 0))
                    dve.wait_ge(ol_done, count(1, pair, par, 0))
                V.tensor_tensor(o32, psO[:, 0, 0:400], rsum, ALU.mult).then_inc(o_done, 1)

            def o_low(st):
                pair, par, b = st
                dve.wait_ge(oh_done, count(1, pair, par, 1))
                at = bass.ds((2 * pair + par) * SQ, SQ)
                V.tensor_tensor(oT[:, 1, :, at], o32.rearrange("p (a q) -> p a q", a=HPG), oT[:, 0, :, at],
                                ALU.subtract).then_inc(ol_done, 1)

            def step(m1, s0, p1, p2, p3):
                if m1:
                    p_low(m1, 2)
                if p2:
                    k_low(p2)
                if p1:
                    maxima(p1, 0)
                if m1:
                    attended(m1)
                if s0:
                    p_high(s0, 0)
                if p1:
                    v_low(p1)
                    maxima(p1, 1)
                    maxima(p1, 2)
                if m1:
                    o_low(m1)
                if p1:
                    for u in range(3, 8):
                        maxima(p1, u)
                    max_split(p1)

            def quant_scale(unit, par):
                dve.wait_ge(quant_ps, unit + 1)
                V.tensor_scalar(wsc[par], psB[:, :, :].rearrange("p a n -> p (a n)"), SCALE_MIN, None, ALU.max
                                ).then_inc(scale_done, 1)
                dve.wait_ge(scale_done, unit + 1)
                V.tensor_tensor(wa2[par], wa2[par], wsc[par], ALU.is_gt).then_inc(mk_done, 1)
                dve.wait_ge(wg_done, unit + 1)
                V.tensor_tensor(wsg[par], wsg[par], wsc[par], ALU.mult).then_inc(sw_done, 1)

            def quant_less(unit, par):
                dve.wait_ge(mk_done, unit + 1)
                dve.wait_ge(sw_done, unit + 1)
                V.tensor_tensor(wsg[par], wsg[par], wa2[par], ALU.mult).then_inc(wh_done, 1)
                dve.wait_ge(wh_done, unit + 1)
                V.tensor_tensor(wsg[par], wsg[par], wb[par], ALU.subtract).then_inc(wd_done, 1)

            def quant(unit, par):
                quant_scale(unit, par)
                quant_less(unit, par)

            pipeline(dve.Fori, step, lambda unit: quant(unit, unit))

            def norm(c, m):
                n = CHUNKS[c]
                V.tensor_tensor(h32[:, m, 0:n], h32[:, m, 0:n], spread_to(c), ALU.mult).then_inc(n_done, 1)

            def norm_low(c, m):
                n = CHUNKS[c]
                dve.wait_ge(nh_done, m + (NM * c + 1))
                V.tensor_tensor(halves(c)[:, 1, m, 0:n], h32[:, m, 0:n], halves(c)[:, 0, m, 0:n], ALU.subtract
                                ).then_inc(nl_done, 1)

            def mean_square(c):
                rows, cols = min(P, CHUNKS[c]), len(TILES[c])
                dve.wait_ge(rms_ps, c + 1)
                if c:
                    dve.wait_ge(rinv_done, c)
                V.tensor_scalar(msq[0:rows, 0:cols], sums_at(c)[0:rows, 0:cols],
                                1.0 / HID, RMS_EPS, ALU.mult, ALU.add).then_inc(rt_done, 1)
                dve.wait_ge(rinv_done, c + 1)
                if c:
                    dve.wait_ge(rb_ps, c)
                for i in range(cols):
                    last = V.tensor_scalar(rdiag[0:rows, i * P:i * P + rows], ident[0:rows, 0:rows],
                                           rinv[0:rows, i:i + 1], ZS, ALU.mult, ALU.mult)
                last.then_inc(rd_done, 1)
                dve.wait_ge(rb_ps, c + 1)
                if c and c < NC - 1:
                    dve.wait_ge(proj_ps, FIRST[c])

            def result(c, tiles=range(4)):
                for T, i, n in tile_list(c):
                    if i not in tiles:
                        continue
                    dve.wait_ge(proj_ps, T + 1)
                    V.scalar_tensor_tensor(out=xs[0:n, c % 2, i, :], in0=psO[0:n, i % 2, :], scalar=1.0 / ZS,
                                           in1=xs[0:n, c % 2, i, :], op0=ALU.mult, op1=ALU.add
                                           ).then_inc(y_done, 1)

            def gated(c, m, par):
                n = CHUNKS[c]
                dve.wait_ge(sil_done, m + (NM * c + 1))
                if c:
                    dve.wait_ge(nl_done, m + (NM * (c - 1) + 1))
                V.scalar_tensor_tensor(out=h32[:, m, 0:n], in0=psW[:, par, 1, 0:n], scalar=1.0 / ZS,
                                       in1=sil[:, par, 0:n], op0=ALU.mult, op1=ALU.mult
                                       ).then_inc(h_done, 1)

            def residual(c, T, i, rows):
                dve.wait_ge(wo_ps, T + 1)
                dve.wait_ge(x_ld[(c % 2) * 4 + i], x_loads(1, c, i))
                V.scalar_tensor_tensor(out=xs[0:rows, c % 2, i, :], in0=psO[0:rows, 0, :], scalar=1.0 / WS,
                                       in1=xs[0:rows, c % 2, i, :], op0=ALU.mult, op1=ALU.add
                                       ).then_inc(x1_done, 1)
                normalise(NT + T, c, i, rows, True)

            def turn_in(c, unit):
                for T, i, rows in tile_list(c):
                    last, more = i == len(TILES[c]) - 1, unit + i < NU
                    residual(c, T, i, rows)
                    if more and not last:
                        quant_scale(unit + i, i % 2)
                    z_of(NT + T, c, i, rows)
                    if more and not last:
                        quant_less(unit + i, i % 2)
                    z_low(NT + T, 1, T * P, rows, ZS, oT)
                    if more and last:
                        quant(unit + i, i % 2)

            def pairs(i, c, unit):
                for par in range(2):
                    gated(c, 2 * i + par, par)
                    quant(unit + par, par)

            def normed(i, c, begin):
                if begin:
                    mean_square(c - 1)
                for j in range(share(c)):
                    norm(c - 1, share(c) * i + j)
                for par in range(2):
                    for j in range(share(c) // 2):
                        norm_low(c - 1, share(c) * i + (share(c) // 2 * par + j))
                    gated(c, 2 * i + par, par)

            def beside(i, c, tile):
                gated(c, 2 * i, 0)
                if tile:
                    T, e, rows = tile
                    residual(c + 1, T, e, rows)
                    z_of(NT + T, c + 1, e, rows)
                    z_low(NT + T, 1, T * P, rows, ZS, oT)
                gated(c, 2 * i + 1, 1)

            dve.wait_ge(oh_done, B)
            dve.wait_ge(ol_done, B)
            dve.wait_ge(v_ps, B)
            feed_forward(dve.Fori, turn_in, pairs, normed, result, beside)
            mean_square(NC - 1)
            dve.wait_ge(w_ready, NU)
            with dve.Fori(0, NM) as m:
                norm(NC - 1, m)
            dve.wait_ge(n_done, NM * NC)
            result(NC - 2, (0,))
            with dve.Fori(0, NM) as m:
                norm_low(NC - 1, m)
            result(NC - 2, (1, 2, 3))
            result(NC - 1)

        @block.tensor
        def _(pe):
            def product(dst, pairs):
                for i, (left, right) in enumerate(pairs):
                    last = nc.tensor.matmul(dst, left, right, start=(i == 0), stop=(i == len(pairs) - 1))
                return last

            HALVES = ((0, 0), (0, 1), (1, 0))

            def turn(k, bank, n):
                pe.wait_ge(z_done, k + 1)
                for kk in range(KC):
                    last = nc.tensor.transpose(psO[:, bank, kk * P:kk * P + n],
                                               zrow[0:n, k % 2, kk * P:(kk + 1) * P], ident[0:n, 0:n])
                last.then_inc(zt_ps, 1)

            def z_in(c, i):
                if c < NC and i < len(TILES[c]):
                    T = FIRST[c] + i
                    if T >= 2:
                        pe.wait_ge(zl_done, T - 1)
                    turn(T, T % 2, TILES[c][i])

            pe.wait_ge(ident_ld, 16)
            for i in range(len(TILES[0])):
                z_in(0, i)
            pe.wait_ge(w_lo, 1)
            for c, cols in enumerate(CHUNKS):
                pe.wait_ge(zl_done, FIRST[c] + len(TILES[c]))
                for hh in range(HPG):
                    if c:
                        pe.wait_ge(ql_done, HPG * (c - 1) + hh + 1)
                    product(psW[:, hh // 2, hh % 2, 0:cols],
                            [(wq_s[:, a, k, hh * P:(hh + 1) * P], zT[c % 2][:, b, k, 0:cols])
                             for k in range(KC) for a, b in HALVES]).then_inc(q_ps, 1)
                    z_in(c + 1, hh)
            pe.wait_ge(const_ld, 16 * 6)

            def k_proj(st):
                pair, par, b = st
                pe.wait_ge(ctxl_done, count(1, pair, par, 1))
                if b == 0:
                    pe.wait_ge(w_lo, 3)
                    pe.wait_ge(ql_done, HPG * NC)
                elif b == 1:
                    pe.wait_ge(kl_done, 1)
                else:
                    pe.wait_ge(max_done, count(8, pair, par, -9))
                product(psW[:, 1, 0, 0:SKP],
                        [(wkv_s[:, a, 0, k, :], ctxs[:, par, h, k, :])
                         for k in range(KC) for a, h in HALVES]).then_inc(k_ps, 1)

            def v_proj(st, t):
                pair, par, b = st
                if b >= 1 and t == 0:
                    pe.wait_ge(max_done, count(8, pair, par, -1))
                last = product(psW[:, 1, 1, t * P:(t + 1) * P],
                               [(ctxs[:, par, h, k, t * P:(t + 1) * P], wkv_s[:, a, 1, k, :])
                                for k in range(KC) for a, h in HALVES])
                if t == KT - 1:
                    last.then_inc(v_ps, 1)

            def score_rows(st, u):
                pair, par, b = st
                if u == 0:
                    pe.wait_ge(k_rd[par], pair * 16 + 16)
                    pe.wait_ge(q_rd[par], pair * 16 + 16)
                    if b >= 1:
                        pe.wait_ge(mc_done, count(1, pair, par, 0))
                elif u == 1:
                    pe.wait_ge(max_done, count(8, pair, par, 1))
                elif u == 2:
                    pe.wait_ge(vl_done, count(1, pair, par, 1))
                    if b < B - 1:
                        pe.wait_ge(kl_done, count(1, pair, par, 2))
                else:
                    pe.wait_ge(max_done, count(8, pair, par, u - 1))
                for e in range(2):
                    n = 2 * u + e
                    last = nc.tensor.matmul(psW[0:SQ, SLOT[u], e, 0:SK], qst[0:ROW_MAX, par, n, :],
                                            kst[0:ROW_MAX, par, n % G, 0:SK], start=True, stop=True)
                last.then_inc(a_ps, 1)

            def max_turn(st):
                pair, par, b = st
                pe.wait_ge(max_done, count(8, pair, par, 8))
                nc.tensor.transpose(psW[0:NH, 0, 0, 0:SQ], mx[0:SQ, :], ident[0:SQ, 0:SQ]).then_inc(mt_ps, 1)

            def score_cols(st, n):
                pair, par, b = st
                t, g = n // G, n % G
                if b == 0 and n < 2:
                    pe.wait_ge(scale_done, EARLY)
                if n == 0:
                    pe.wait_ge(m_rd[par], pair * 32 + 32)
                if n >= 2 or b >= 1:
                    pe.wait_ge(exp_done, count(12, pair, par, n - 1))
                nc.tensor.matmul(psB[:, n % 2, 0:400], kst[:, par, g, t * P:(t + 1) * P],
                                 qst[:, par, :, :].rearrange("p (a g) q -> p a g q", g=G)[:, :, g, :],
                                 start=True, stop=True).then_inc(b_ps, 1)

            def attend(st, t):
                pair, par, b = st
                if t == 0:
                    pe.wait_ge(vl_done, count(1, pair, par, 1))
                    if b >= 1:
                        pe.wait_ge(o_done, count(1, pair, par, 0))
                if t < 2:
                    pe.wait_ge(pl_p, count(2, pair, par, t + 1))
                else:
                    pe.wait_ge(pl_v, count(1, pair, par, 1))
                ones = key_ones[:, 1 if t == KT - 1 else 0, :]
                for bank, half, probs in ((0, 0, ph), (0, 0, pl), (0, 1, ph), (1, None, ph), (1, None, pl)):
                    for g in range(G):
                        left = ones if half is None else vs[:, par, half, t, g * DH:(g + 1) * DH]
                        last = nc.tensor.matmul(
                            psO[g * DH:(g + 1) * DH, bank, 0:400], left, probs[:, t, g, :],
                            start=(t == 0 and probs is ph and half != 1),
                            stop=(t == KT - 1 and (half == 1 or (half is None and probs is pl))))
                last.then_inc(pv_done, 1)

            def step(m1, s0, p1, p2, p3):
                if p2:
                    k_proj(p2)
                n = u = v = 0
                for what in "1 A 2 B B V B V B V A B B A A B B A B B A B A B A 0 T".split():
                    if what == "B":
                        if s0:
                            score_cols(s0, n)
                        n += 1
                    elif what == "A":
                        if p1:
                            score_rows(p1, u)
                        u += 1
                    elif what == "V":
                        if p1:
                            v_proj(p1, v)
                        v += 1
                    elif what == "T":
                        if p1:
                            max_turn(p1)
                    elif what == "0":
                        if s0:
                            attend(s0, 0)
                    elif m1:
                        attend(m1, int(what))

            def scales(unit, par):
                pe.wait_ge(wa_done, unit + 1)
                if isinstance(unit, int) and unit == EARLY:
                    pe.wait_ge(exp_done, 12 * B)
                if not (isinstance(unit, int) and unit == 0):
                    pe.wait_ge(scale_done, unit)
                for e in range(2):
                    last = nc.tensor.matmul(psB[:, e, :], block64[:, :], wa2[par][:, e * 512:(e + 1) * 512],
                                            start=True, stop=True)
                last.then_inc(quant_ps, 1)

            pipeline(pe.Fori, step, lambda unit: scales(unit, unit))

            def project(T, c, i, n):
                pe.wait_ge(w_lo, 4)
                if T:
                    pe.wait_ge(x1_done, T)
                if T == 0:
                    pe.wait_ge(ol_done, B)
                if c >= 2:
                    pe.wait_ge(y_done, FIRST[c - 1])
                at = c * CH + i * P
                product(psO[0:n, 0, :], [(oT[:, a, k, at:at + n], wo_s[:, b, k, :])
                                         for k in range(KC) for a, b in HALVES]).then_inc(wo_ps, 1)

            def square_sums(c):
                pe.wait_ge(acc_done, NM * (c + 1))
                if c < NC - 1:
                    pe.wait_ge(zl_done, NT + chunk_end(c + 1))
                    pe.wait_ge(y_done, FIRST[c])
                else:
                    pe.wait_ge(h_done, NM * NC)
                for i, n in enumerate(TILES[c]):
                    last = nc.tensor.matmul(sums_at(c)[0:n, i:i + 1], acc[:, i * P:i * P + n], onesf[:, 0:1],
                                            start=True, stop=True)
                last.then_inc(rms_ps, 1)

            def spread(c):
                rows = min(P, CHUNKS[c])
                pe.wait_ge(rd_done, c + 1)
                nc.tensor.matmul(spread_to(c), onesf[0:rows, :], rdiag[0:rows, 0:CHUNKS[c]],
                                 start=True, stop=True).then_inc(rb_ps, 1)

            def down(c, between=None):
                pe.wait_ge(w_ready, NU)
                pe.wait_ge(nl_done, NM * (c + 1))
                pe.wait_ge(x1_done, chunk_end(min(c + 1, NC - 1)))
                pe.wait_ge(zl_done, NT + chunk_end(min(c + 1, NC - 1)))
                pe.wait_ge(rt_done, c + 1)
                for T, i, n in tile_list(c):
                    if T:
                        pe.wait_ge(y_done, T if i == 0 else T - 1)
                    product(psO[0:n, i % 2, :],
                            [(halves(c)[:, h, m, i * P:i * P + n],
                              w_ffn[:, NU_GU + m // 2, (m % 2) * D:(m % 2 + 1) * D])
                             for m in range(NM) for h in range(2)]).then_inc(proj_ps, 1)
                    if i == 0 and between:
                        between()

            def turn_tile(c, T, n):
                if T:
                    pe.wait_ge(zl_done, NT + T)
                if c >= 2:
                    pe.wait_ge(y_done, FIRST[c - 1])
                    pe.wait_ge(rt_done, c - 1)
                turn(NT + T, 1, n)

            def gate_up(c, m, par):
                n = CHUNKS[c]
                if not starts(c, m, 2):
                    pe.wait_ge(h_done, m + (NM * c - 1))
                if c == 0:
                    pe.wait_ge(w_ready, m + 1)
                for e in range(2):
                    last = product(psW[:, par, e, 0:n],
                                   [(w_ffn[:, m, k * 256 + e * P:k * 256 + (e + 1) * P],
                                     oT[:, h, k, c * CH:c * CH + n]) for k in range(KC) for h in range(2)])
                last.then_inc(gu_ps, 1)

            def turn_in(c, unit):
                tiles = tile_list(c)
                project(tiles[0][0], c, *tiles[0][1:])
                for e, (T, i, rows) in enumerate(tiles):
                    if unit + i < NU:
                        scales(unit + i, i % 2)
                    if e + 1 < len(tiles):
                        T1, i1, rows1 = tiles[e + 1]
                        project(T1, c, i1, rows1)
                    turn_tile(c, T, rows)
                pe.wait_ge(zl_done, NT + chunk_end(c))
                if c == 0:
                    pe.wait_ge(mc_done, B)

            def pairs(i, c, unit):
                for par in range(2):
                    gate_up(c, 2 * i + par, par)
                    scales(unit + par, par)

            def normed(i, c, begin):
                if begin:
                    pe.wait_ge(zl_done, NT + chunk_end(c))
                    if c == 1:
                        square_sums(0)
                    gate_up(c, 0, 0)
                    if c > 1:
                        square_sums(c - 1)
                    spread(c - 1)
                    gate_up(c, 1, 1)
                else:
                    for par in range(2):
                        gate_up(c, 2 * i + par, par)

            def beside(i, c, tile):
                gate_up(c, 2 * i, 0)
                if tile:
                    project(tile[0], c + 1, *tile[1:])
                gate_up(c, 2 * i + 1, 1)
                if tile:
                    turn_tile(c + 1, tile[0], tile[2])

            feed_forward(pe.Fori, turn_in, pairs, normed, down, beside)
            square_sums(NC - 1)
            down(NC - 2, lambda: spread(NC - 1))
            down(NC - 1)


_OUTS = [((B, SQ, D), "float32")]


def constants():
    f16 = np.float16
    slope = np.float32(2.0 ** (-8.0 / NH)) ** np.arange(1, NH + 1, dtype=np.float32)
    order = [g * HPG + a for a in range(HPG) for g in range(G)]
    slope = slope[order].astype(np.float64)
    qaux = np.zeros((P - ROW_AUX, NH, SQ), f16)
    off = -slope[:, None] * np.arange(SQ)[None, :]
    for row, v in ((0, np.repeat(slope[:, None], SQ, 1)), (3, off)):
        hi = v.astype(f16)
        lo = (v - hi.astype(np.float64)).astype(f16)
        if row == 0:
            qaux[0], qaux[1] = hi, lo
        else:
            qaux[3], qaux[4] = hi, lo
    qaux[2] = MASK_Q
    kaux = np.zeros((P - ROW_AUX, G, SKP), f16)
    for row in (3, 4, ROW_MAX - ROW_AUX, ROW_MAX - ROW_AUX + 1):
        kaux[row, :, :SK] = 1.0
    kpos = np.zeros((B, SKP), f16)
    kpos[:, :SK] = np.arange(SK)
    key_ones = np.ones((P, 2, DH), f16)
    key_ones[SK - (KT - 1) * P:, 1] = 0.0
    block = np.kron(np.eye(2), np.full((64, 64), 2.0 ** -7)).astype(f16)
    return {"qaux": qaux, "kaux": kaux, "kpos": kpos, "ident": np.eye(P, dtype=np.float32),
            "block64": block, "key_ones": key_ones}


def layouts(x, ctx_2048, mask_BxS2_bf1, L0_xattn_Wq, L0_xattn_Wk, L0_xattn_Wv, L0_xattn_Wo,
            L0_ffn_w_gate_up, L0_ffn_w_proj):
    def rows(w):
        return w.reshape(KC, P, -1).transpose(1, 0, 2)

    wq = L0_xattn_Wq.reshape(KC, P, G, HPG, DH).transpose(1, 0, 3, 2, 4).reshape(P, KC, D)
    wo = L0_xattn_Wo.reshape(G, HPG, DH, D).transpose(0, 2, 1, 3).reshape(P, HPG, D)
    gu = L0_ffn_w_gate_up.reshape(2, NM, P, KC, P).transpose(1, 4, 3, 0, 2).reshape(NM, P, UNIT)
    p = L0_ffn_w_proj.reshape(D, NM // 2, 2, P).transpose(1, 3, 2, 0).reshape(NM // 2, P, UNIT)
    return {"x": x, "ctxT": ctx_2048.reshape(B, SK, KC, P).transpose(0, 3, 2, 1),
            "mask": mask_BxS2_bf1.view(np.uint8), "wq": wq, "wk": rows(L0_xattn_Wk),
            "wv": rows(L0_xattn_Wv), "wo": wo, "w_gu": gu, "w_p": p}


def kernel(**inputs):
    import concourse.bacc as _bacc
    from concourse.bass_utils import run_bass_kernel_spmd as _run

    nc = _bacc.Bacc("TRN2", target_bir_lowering=False, num_devices=1)
    arrays, args = {}, []
    for name, a in {**layouts(**{k: np.asarray(v) for k, v in inputs.items()}), **constants()}.items():
        a = np.ascontiguousarray(a)
        arrays[f"in_{name}"] = a
        args.append(nc.dram_tensor(f"in_{name}", a.shape, mybir.dt.from_np(a.dtype), kind="ExternalInput").ap())
    for i, (shape, dtype) in enumerate(_OUTS):
        args.append(nc.dram_tensor(f"out_{i}", shape, mybir.dt.from_np(np.dtype(dtype)), kind="ExternalOutput").ap())
    xattn_ffn(nc, *args)
    r = _run(nc, [arrays], core_ids=[0])
    return r.results[0]["out_0"]
```
